# Optimizing a Trainium2 kernel written in Bass

```python
import numpy as np
import jax
import jax.numpy as jnp

def _softmax(x, axis=-1):
    return jax.nn.softmax(x, axis=axis)

def _gelu(x):
    return jax.nn.gelu(x, approximate=True)

def _silu(x):
    return jax.nn.silu(x)

def _sigmoid(x):
    return jax.nn.sigmoid(x)

def _layernorm(x, axis=-1, eps=1e-05):
    m = jnp.mean(x, axis=axis, keepdims=True)
    v = jnp.var(x, axis=axis, keepdims=True)
    return (x - m) / jnp.sqrt(v + eps)

def _scatter_add(tgt, idx, src, axis=0):
    return tgt.at[idx].add(src)

def _segment_sum(src, seg, n):
    return jax.ops.segment_sum(src, seg, n)
kernel_name = 'mk_audio_tower_d1_tok_audfeat256_r4_729b77'

def setup_inputs(seed: int=0):
    np.random.seed(seed)
    _w = jnp.asarray

    def _rec_inputs():
        import jax
        import jax.numpy as jnp
        _rk = jax.random.key(seed)
        x = -0.000392918 + 0.999932 * jax.random.normal(jax.random.fold_in(_rk, 1), (64, 250, 64), jnp.float32)
        return x
    x = _rec_inputs()

    def _L0_tok_setup():
        import jax, jax.numpy as jnp
        import numpy as np
        from jax import lax
        B, S, CIN, COUT, K = (32, 512, 64, 64, 16)
        key = jax.random.key(seed)
        k1, k2, k3, k4 = jax.random.split(key, 4)
        x = jax.random.normal(k1, (B, S, CIN), dtype=jnp.float32)
        w_real = jax.random.normal(k2, (COUT, CIN, K), dtype=jnp.float32) * 0.1
        w_imag = jax.random.normal(k3, (COUT, CIN, K), dtype=jnp.float32) * 0.1
        phases = jax.random.normal(k4, (K,), dtype=jnp.float32) * 0.1
        return {'x': x, 'w_real': w_real, 'w_imag': w_imag, 'phases': phases}
    _L0_tok_all = _L0_tok_setup()
    _L0_tok_in = {k: v for k, v in _L0_tok_all.items() if k in ('w_real', 'w_imag', 'phases')}
    del _L0_tok_all

    def _L0_attn_setup():
        import jax, jax.numpy as jnp
        import numpy as np
        B, V = (8, 100)
        D_MODEL, D_STATE, N_LAYERS = (64, 64, 2)
        D_INNER, DT_RANK, K_CONV = (128, 16, 4)

        def _silu(z):
            return z * jax.nn.sigmoid(z)

        def _layernorm(z, w, b, eps=1e-05):
            mu = jnp.mean(z, axis=-1, keepdims=True)
            var = jnp.mean((z - mu) ** 2, axis=-1, keepdims=True)
            return (z - mu) * jax.lax.rsqrt(var + eps) * w + b

        def _ssm_block(x, lw, lb, iw, ib, cw, cb, xw, dw, db, alog, dpar, ow, ob):
            N, L, _ = x.shape
            res = x
            xn = _layernorm(x, lw, lb)
            xr = xn @ iw + ib
            xs, gate = jnp.split(xr, 2, axis=-1)
            rhs = cw[:, None, :]
            xc = jax.lax.conv_general_dilated(xs, rhs, window_strides=(1,), padding=[(K_CONV - 1, 0)], dimension_numbers=('NWC', 'WIO', 'NWC'), feature_group_count=D_INNER) + cb
            xc = _silu(xc)
            dbl = xc @ xw
            dt = dbl[..., :DT_RANK]
            Bm = dbl[..., DT_RANK:DT_RANK + D_STATE]
            Cm = dbl[..., DT_RANK + D_STATE:]
            dt = jax.nn.softplus(dt @ dw + db)
            A = -jnp.exp(alog)
            dA = jnp.exp(jnp.einsum('nld,ds->nlds', dt, A))
            dBx = jnp.einsum('nld,nls,nld->nlds', dt, Bm, xc)

            def step(h, inp):
                dA_t, dBx_t, C_t = inp
                h = dA_t * h + dBx_t
                y = jnp.einsum('nds,ns->nd', h, C_t)
                return (h, y)
            h0 = jnp.zeros((N, D_INNER, D_STATE), x.dtype)
            _, ys = jax.lax.scan(step, h0, (dA.transpose(1, 0, 2, 3), dBx.transpose(1, 0, 2, 3), Cm.transpose(1, 0, 2)))
            y = ys.transpose(1, 0, 2)
            y = y + dpar * xc
            y = y * _silu(gate)
            return y @ ow + ob + res
        key = jax.random.key(seed)
        ks = jax.random.split(key, 8)
        f32 = jnp.float32

        def rn(k, shape, scale=0.02):
            return jax.random.normal(k, shape, dtype=f32) * scale
        return {'x': jax.random.normal(ks[0], (B, V, D_MODEL), dtype=f32), 'ln_w': jnp.ones((N_LAYERS, D_MODEL), f32), 'ln_b': jnp.zeros((N_LAYERS, D_MODEL), f32), 'in_w': rn(ks[1], (N_LAYERS, D_MODEL, 2 * D_INNER)), 'in_b': jnp.zeros((N_LAYERS, 2 * D_INNER), f32), 'conv_w': rn(ks[2], (N_LAYERS, K_CONV, D_INNER), 0.1), 'conv_b': jnp.zeros((N_LAYERS, D_INNER), f32), 'xproj_w': rn(ks[3], (N_LAYERS, D_INNER, DT_RANK + 2 * D_STATE)), 'dtproj_w': rn(ks[4], (N_LAYERS, DT_RANK, D_INNER)), 'dtproj_b': rn(ks[5], (N_LAYERS, D_INNER), 0.1), 'A_log': jnp.log(jnp.tile(jnp.arange(1, D_STATE + 1, dtype=f32)[None, None, :], (N_LAYERS, D_INNER, 1))), 'D_param': jnp.ones((N_LAYERS, D_INNER), f32), 'out_w': rn(ks[6], (N_LAYERS, D_INNER, D_MODEL)), 'out_b': jnp.zeros((N_LAYERS, D_MODEL), f32)}
    _L0_attn_all = _L0_attn_setup()
    _L0_attn_in = {k: v for k, v in _L0_attn_all.items() if k in ('ln_w', 'ln_b', 'in_w', 'in_b', 'conv_w', 'conv_b', 'xproj_w', 'dtproj_w', 'dtproj_b', 'A_log', 'D_param', 'out_w', 'out_b')}
    del _L0_attn_all

    def _L0_ffn_setup():
        import jax, jax.numpy as jnp
        import numpy as np
        B, T, D, H, E = (16, 1024, 64, 128, 8)
        key = jax.random.key(seed)
        ks = jax.random.split(key, 5)
        x = jax.random.normal(ks[0], (B, T, D), dtype=jnp.float32)
        gate_w = jax.random.normal(ks[1], (D, E), dtype=jnp.float32) * 0.02
        gate_b = jnp.zeros((E,), dtype=jnp.float32)
        W1 = jax.random.normal(ks[2], (E, D, H), dtype=jnp.float32) * 0.02
        b1 = jnp.zeros((E, H), dtype=jnp.float32)
        W2 = jax.random.normal(ks[3], (E, H, D), dtype=jnp.float32) * 0.02
        b2 = jnp.zeros((E, D), dtype=jnp.float32)
        return {'x': x, 'gate_w': gate_w, 'gate_b': gate_b, 'W1': W1, 'b1': b1, 'W2': W2, 'b2': b2}
    _L0_ffn_all = _L0_ffn_setup()
    _L0_ffn_in = {k: v for k, v in _L0_ffn_all.items() if k in ('gate_w', 'gate_b', 'W1', 'b1', 'W2', 'b2')}
    del _L0_ffn_all
    return {'x': x, 'L0_tok_w_real': _L0_tok_in['w_real'], 'L0_tok_w_imag': _L0_tok_in['w_imag'], 'L0_tok_phases': _L0_tok_in['phases'], 'L0_attn_ln_w': _L0_attn_in['ln_w'], 'L0_attn_ln_b': _L0_attn_in['ln_b'], 'L0_attn_in_w': _L0_attn_in['in_w'], 'L0_attn_in_b': _L0_attn_in['in_b'], 'L0_attn_conv_w': _L0_attn_in['conv_w'], 'L0_attn_conv_b': _L0_attn_in['conv_b'], 'L0_attn_xproj_w': _L0_attn_in['xproj_w'], 'L0_attn_dtproj_w': _L0_attn_in['dtproj_w'], 'L0_attn_dtproj_b': _L0_attn_in['dtproj_b'], 'L0_attn_A_log': _L0_attn_in['A_log'], 'L0_attn_D_param': _L0_attn_in['D_param'], 'L0_attn_out_w': _L0_attn_in['out_w'], 'L0_attn_out_b': _L0_attn_in['out_b'], 'L0_ffn_gate_w': _L0_ffn_in['gate_w'], 'L0_ffn_gate_b': _L0_ffn_in['gate_b'], 'L0_ffn_W1': _L0_ffn_in['W1'], 'L0_ffn_b1': _L0_ffn_in['b1'], 'L0_ffn_W2': _L0_ffn_in['W2'], 'L0_ffn_b2': _L0_ffn_in['b2']}

def reference(x, L0_tok_w_real, L0_tok_w_imag, L0_tok_phases, L0_attn_ln_w, L0_attn_ln_b, L0_attn_in_w, L0_attn_in_b, L0_attn_conv_w, L0_attn_conv_b, L0_attn_xproj_w, L0_attn_dtproj_w, L0_attn_dtproj_b, L0_attn_A_log, L0_attn_D_param, L0_attn_out_w, L0_attn_out_b, L0_ffn_gate_w, L0_ffn_gate_b, L0_ffn_W1, L0_ffn_b1, L0_ffn_W2, L0_ffn_b2):
    import jax
    import jax.numpy as jnp

    def _L0_tok_ref(x, w_real, w_imag, phases):
        import jax, jax.numpy as jnp
        import numpy as np
        from jax import lax
        B, S, CIN, COUT, K = (32, 512, 64, 64, 16)
        w_eff = jnp.cos(phases)[None, None, :] * w_real - jnp.sin(phases)[None, None, :] * w_imag
        y = lax.conv_general_dilated(jnp.transpose(x, (0, 2, 1)), w_eff, window_strides=(1,), padding='VALID', dimension_numbers=('NCH', 'OIH', 'NCH'))
        return jnp.transpose(y, (0, 2, 1))

    def _L0_attn_ref(x, ln_w, ln_b, in_w, in_b, conv_w, conv_b, xproj_w, dtproj_w, dtproj_b, A_log, D_param, out_w, out_b):
        import jax, jax.numpy as jnp
        import numpy as np
        B, V = (8, 100)
        D_MODEL, D_STATE, N_LAYERS = (64, 64, 2)
        D_INNER, DT_RANK, K_CONV = (128, 16, 4)

        def _silu(z):
            return z * jax.nn.sigmoid(z)

        def _layernorm(z, w, b, eps=1e-05):
            mu = jnp.mean(z, axis=-1, keepdims=True)
            var = jnp.mean((z - mu) ** 2, axis=-1, keepdims=True)
            return (z - mu) * jax.lax.rsqrt(var + eps) * w + b

        def _ssm_block(x, lw, lb, iw, ib, cw, cb, xw, dw, db, alog, dpar, ow, ob):
            N, L, _ = x.shape
            res = x
            xn = _layernorm(x, lw, lb)
            xr = xn @ iw + ib
            xs, gate = jnp.split(xr, 2, axis=-1)
            rhs = cw[:, None, :]
            xc = jax.lax.conv_general_dilated(xs, rhs, window_strides=(1,), padding=[(K_CONV - 1, 0)], dimension_numbers=('NWC', 'WIO', 'NWC'), feature_group_count=D_INNER) + cb
            xc = _silu(xc)
            dbl = xc @ xw
            dt = dbl[..., :DT_RANK]
            Bm = dbl[..., DT_RANK:DT_RANK + D_STATE]
            Cm = dbl[..., DT_RANK + D_STATE:]
            dt = jax.nn.softplus(dt @ dw + db)
            A = -jnp.exp(alog)
            dA = jnp.exp(jnp.einsum('nld,ds->nlds', dt, A))
            dBx = jnp.einsum('nld,nls,nld->nlds', dt, Bm, xc)

            def step(h, inp):
                dA_t, dBx_t, C_t = inp
                h = dA_t * h + dBx_t
                y = jnp.einsum('nds,ns->nd', h, C_t)
                return (h, y)
            h0 = jnp.zeros((N, D_INNER, D_STATE), x.dtype)
            _, ys = jax.lax.scan(step, h0, (dA.transpose(1, 0, 2, 3), dBx.transpose(1, 0, 2, 3), Cm.transpose(1, 0, 2)))
            y = ys.transpose(1, 0, 2)
            y = y + dpar * xc
            y = y * _silu(gate)
            return y @ ow + ob + res
        b, v, s = x.shape
        h = x.reshape(b * v, 1, s)
        for i in range(N_LAYERS):
            h = _ssm_block(h, ln_w[i], ln_b[i], in_w[i], in_b[i], conv_w[i], conv_b[i], xproj_w[i], dtproj_w[i], dtproj_b[i], A_log[i], D_param[i], out_w[i], out_b[i])
        return h.reshape(b, v, D_MODEL)

    def _L0_ffn_ref(x, gate_w, gate_b, W1, b1, W2, b2):
        import jax, jax.numpy as jnp
        import numpy as np
        B, T, D, H, E = (16, 1024, 64, 128, 8)
        Bb, Tt, Dd = x.shape
        Ee = gate_w.shape[1]
        xf = x.reshape(-1, Dd)
        N = xf.shape[0]
        logits = xf @ gate_w + gate_b
        probs = jax.nn.softmax(logits, axis=-1)
        top2_vals, top2_idx = jax.lax.top_k(probs, 2)
        cw = jnp.zeros((N, Ee), dtype=xf.dtype).at[jnp.arange(N)[:, None], top2_idx].add(top2_vals)

        def step(acc, params):
            w1, bb1, w2, bb2, we = params
            h = jax.nn.gelu(xf @ w1 + bb1, approximate=False)
            y = h @ w2 + bb2
            return (acc + we[:, None] * y, None)
        out, _ = jax.lax.scan(step, jnp.zeros_like(xf), (W1, b1, W2, b2, cw.T))
        return out.reshape(Bb, Tt, Dd)
    h = _L0_tok_ref(x, L0_tok_w_real, L0_tok_w_imag, L0_tok_phases)
    h = h + _L0_attn_ref(_layernorm(h, axis=-1), L0_attn_ln_w, L0_attn_ln_b, L0_attn_in_w, L0_attn_in_b, L0_attn_conv_w, L0_attn_conv_b, L0_attn_xproj_w, L0_attn_dtproj_w, L0_attn_dtproj_b, L0_attn_A_log, L0_attn_D_param, L0_attn_out_w, L0_attn_out_b)
    h = h + _L0_ffn_ref(_layernorm(h, axis=-1), L0_ffn_gate_w, L0_ffn_gate_b, L0_ffn_W1, L0_ffn_b1, L0_ffn_W2, L0_ffn_b2)
    return h

_drawn_inputs = setup_inputs


def setup_inputs(seed=0):
    import zlib

    import numpy as np

    out = dict(_drawn_inputs(seed))
    spreads = {'L0_attn_ln_w': (1.0, 0.6),
     'L0_attn_ln_b': (0.0, 0.8),
     'L0_attn_in_b': (0.0, 0.8),
     'L0_attn_conv_b': (0.0, 0.8),
     'L0_attn_D_param': (1.0, 0.6),
     'L0_attn_out_b': (0.0, 0.8),
     'L0_ffn_gate_b': (0.0, 2.0),
     'L0_ffn_b1': (0.0, 2.0),
     'L0_ffn_b2': (0.0, 2.0)}
    factors = {'L0_attn_in_w': 8.0,
     'L0_attn_conv_w': 8.0,
     'L0_attn_xproj_w': 8.0,
     'L0_attn_dtproj_w': 8.0,
     'L0_attn_dtproj_b': 8.0,
     'L0_attn_out_w': 8.0,
     'L0_ffn_gate_w': 64.0,
     'L0_ffn_W1': 64.0,
     'L0_ffn_W2': 64.0}
    for name, (base, spread) in spreads.items():
        noise = np.random.default_rng([zlib.crc32(name.encode()), seed]).standard_normal(out[name].shape)
        drawn = base * np.exp(spread * noise) if base else spread * noise
        out[name] = jnp.asarray(drawn.astype(out[name].dtype))
    for name, factor in factors.items():
        out[name] = (out[name] * factor).astype(out[name].dtype)
    return out
```

```python
from contextlib import ExitStack

import concourse.bass as bass
from concourse import mybir

ALU = mybir.AluOpType
ACT = mybir.ActivationFunctionType
AX = mybir.AxisListType
F32 = mybir.dt.float32
F32R = mybir.dt.float32r

EPS = 1e-5
PI = 3.14159265358979
ROUND = 12582912.0
TWO_PI_HI = 6.28125
TWO_PI_LO = 1.9353071795864769e-3
SOFTPLUS_CAP = 1e18
LOGIT_DROP = -3.0e38


def audio_tower(nc, x, w_real, w_imag, phases, ln_w, ln_b, in_w, in_b, conv_w, conv_b, xproj_w,
                dtproj_w, dtproj_b, D_param, out_w, out_b, gate_w, gate_b, W1, b1, W2, b2, out):
    B, S, CIN = x.shape
    COUT, _, K = w_real.shape
    SO = S - K + 1
    NL, D, DI2 = in_w.shape
    DI = DI2 // 2
    DS = (xproj_w.shape[2] - dtproj_w.shape[1]) // 2
    RK = dtproj_w.shape[1]
    E, _, H = W1.shape
    G = 4
    NCH = B // G
    UI = S // 2
    U = (SO + 1) // 2
    JT = K // 2 + 1
    NB = 2 * G
    HALF = NB // 2 * U
    TD = NB * D
    EP = 128 // NB

    xv = x.rearrange("b (v c) i -> v b (c i)", c=2)
    out_pairs = out[:, 0:2 * (U - 1), :].rearrange("b (u c) d -> u b (c d)", c=2)
    out_last = out[:, 2 * (U - 1):SO, :].rearrange("b c d -> c b d")

    with ExitStack() as ctx:
        def sb(name, shape, dt=F32):
            return ctx.enter_context(nc.sbuf_tensor(name, shape, dt))

        def sem(name):
            return ctx.enter_context(nc.semaphore(name))

        bank = [ctx.enter_context(nc.psum_tensor(f"bank{i}", [128, 512], F32)) for i in range(8)]
        HEAD = bank[0]
        RING = [[bank[1], bank[2]], [bank[3], bank[4]]]
        HID = [bank[5], bank[6]]
        YB = bank[7]

        ident = sb("ident", [128, 128])
        NV = 8 * NL + E
        vrow = sb("vrow", [NV, 128])
        vcol = sb("vcol", [128, NV])
        inb = vcol[:, 0:2 * NL].rearrange("d (l h) -> d l h", l=NL)
        tapw, tapb, dpb, dpar = (vcol[:, (2 + i) * NL:(3 + i) * NL] for i in range(4))
        b1c = vcol[:, 6 * NL:6 * NL + E]
        lnw, lnb = (vcol[:, 6 * NL + E + i * NL:6 * NL + E + (i + 1) * NL] for i in range(2))
        wr_s = sb("wr_s", [COUT, CIN * K])
        wi_s = sb("wi_s", [COUT, CIN * K])
        ph = sb("ph", [COUT, 2, K])
        phk = sb("phk", [COUT, 2, K])
        cs = sb("cs", [COUT, 2, K])
        wk = sb("wk", [COUT, K + 3, CIN])
        wk2 = sb("wk2", [COUT, K, CIN])
        cwf = sb("cwf", [128, JT, 128])
        cwh = sb("cwh", [128, JT, 128], F32R)
        cwl = sb("cwl", [128, JT, 128], F32R)
        inw = sb("inw", [128, NL, DI2])
        inf = sb("inf", [128, NL, DI2])
        inh = sb("inh", [128, NL, DI2], F32R)
        inl = sb("inl", [128, NL, DI2], F32R)
        bias_g = sb("bias_g", [DI, NL])
        bias_s = sb("bias_s", [DI, NL])
        bias_x = sb("bias_x", [DI, NL])
        xpw = sb("xpw", [DI, NL, RK + 2 * DS])
        xpT = sb("xpT", [RK, NL, DI])
        dpw = sb("dpw", [RK, NL, DI])
        wdt = sb("wdt", [DI, NL, DI])
        ow = sb("ow", [DI, NL, D])
        owd = sb("owd", [DI, NL, D])
        obr = sb("obr", [U, NL, D])
        gwf = sb("gwf", [128, E])
        gwh = sb("gwh", [128, E], F32R)
        gwl = sb("gwl", [128, E], F32R)
        gbr = sb("gbr", [U, E])
        rank = sb("rank", [U, E])
        w1f = sb("w1f", [128, E, H])
        w1h = sb("w1h", [128, E, H], F32R)
        w1l = sb("w1l", [128, E, H], F32R)
        w2s = sb("w2s", [H, E, D])
        b2d = sb("b2d", [128, NB, D])
        nhalf = sb("nhalf", [U, NB])
        inv_d = sb("inv_d", [U, NB])
        eps = sb("eps", [U, NB])
        r1m = sb("r1m", [U, NB])

        xs = sb("xs", [UI, G, 128])
        xh = sb("xh", [128, G, UI + 1], F32R)
        xl = sb("xl", [128, G, UI + 1], F32R)
        cf = sb("cf", [128, G, U])
        ct = sb("ct", [U, TD])
        lnsum = sb("lnsum", [U, 3, NB])
        lnd = sb("lnd", [U, 3, TD])
        lnsq = sb("lnsq", [U, 3, TD])
        lnvar = sb("lnvar", [U, 3, NB])
        lnve = sb("lnve", [U, 3, NB])
        lnr = sb("lnr", [U, 3, NB])
        r1q = sb("r1q", [U, NB])
        r1v = sb("r1v", [U, NB])
        r1w = sb("r1w", [U, NB])
        r2 = sb("r2", [U, NB])
        r12 = sb("r12", [U, NB])
        lna = sb("lna", [U, 3, TD])
        lhl = sb("lhl", [U, 3, NB, 2 * D])
        base = sb("base", [U, 2, TD])
        base_t = sb("base_t", [U, 2, TD])
        at = [sb(f"at{i}", [128, 2 * HALF], F32R) for i in range(3)]
        xc = [sb(f"xc{i}", [DI, 2 * HALF]) for i in range(2)]
        sg = [sb(f"sg{i}", [DI, 2 * HALF]) for i in range(2)]
        u0 = [sb(f"u0{i}", [DI, 2 * HALF]) for i in range(2)]
        ex = [sb(f"ex{i}", [DI, 2 * HALF]) for i in range(2)]
        dt = [sb(f"dt{i}", [DI, 2 * HALF]) for i in range(2)]
        bm = [sb(f"bm{i}", [U, NB, DS]) for i in range(2)]
        bcp = [sb(f"bcp{i}", [U, NB, DS]) for i in range(2)]
        bc = [sb(f"bc{i}", [U, NB]) for i in range(2)]
        zy = [sb(f"zy{i}", [U, TD]) for i in range(2)]
        zb = [sb(f"zb{i}", [U, TD]) for i in range(2)]
        z = [sb(f"z{i}", [U, TD]) for i in range(2)]
        lgt = sb("lgt", [U, NB, E])
        lmx = sb("lmx", [U, NB])
        leq = sb("leq", [U, NB, E])
        lcd = sb("lcd", [U, NB, E])
        lkx = sb("lkx", [U, NB])
        lhot = sb("lhot", [U, NB, E])
        lg2 = sb("lg2", [U, NB, E])
        lmx2 = sb("lmx2", [U, NB])
        leq2 = sb("leq2", [U, NB, E])
        lcd2 = sb("lcd2", [U, NB, E])
        lkx2 = sb("lkx2", [U, NB])
        lhot2 = sb("lhot2", [U, NB, E])
        lsel = sb("lsel", [U, NB, E])
        lsh = sb("lsh", [U, NB, E])
        lex = sb("lex", [U, NB, E])
        lsm = sb("lsm", [U, NB])
        lrc = sb("lrc", [U, NB])
        lpw = sb("lpw", [U, NB, E])
        cwt = sb("cwt", [U, NB, EP])
        cwT = sb("cwT", [128, U])
        gl = [sb(f"gl{i}", [H, 2 * HALF]) for i in range(2)]
        py = [sb(f"py{i}", [U, TD]) for i in range(2)]
        acc = sb("acc", [U, TD])

        s_w = sem("weights_in")
        s_id = sem("ident_ready")
        s_pz = sem("pool_consts")
        v_w = sem("dve_weight_step")
        angles_ready = sem("angles_ready")
        sin_ready = sem("sin_ready")
        vcol_done = sem("vcol_done")
        vcol_ready = sem("vcol_ready")
        wk_ready = sem("wk_ready")
        cwp_done = sem("cwp_done")
        xpT_done = sem("xpT_done")
        xpT_ready = sem("xpT_ready")
        inbias_done = sem("inbias_done")
        wdt_done = sem("wdt_done")
        weights_ready = sem("weights_ready")
        s_x = sem("x_in")
        s_out = sem("out_stored")
        xt_ready = sem("xt_ready")
        xh_ready = sem("xh_ready")
        xl_ready = sem("xl_ready")
        conv_done = sem("conv_done")
        cf_ready = sem("cf_ready")
        t1_done = sem("t1_done")
        c_saved = sem("c_saved")
        ln_sum = [sem(f"ln_sum{i}") for i in range(3)]
        ln_d = [sem(f"ln_d{i}") for i in range(3)]
        ln_sq = [sem(f"ln_sq{i}") for i in range(3)]
        ln_ve = [sem(f"ln_ve{i}") for i in range(3)]
        ln_var = [sem(f"ln_var{i}") for i in range(3)]
        ln_small = [sem(f"ln_small{i}") for i in range(3)]
        ln_a = [sem(f"ln_a{i}") for i in range(3)]
        ln_hi = [sem(f"ln_hi{i}") for i in range(3)]
        ln_lo = [sem(f"ln_lo{i}") for i in range(3)]
        base_part = [sem(f"base_part{i}") for i in range(2)]
        base_ready = [sem(f"base_ready{i}") for i in range(2)]
        t2_done = [sem(f"t2_done{i}") for i in range(3)]
        at_a = [sem(f"at_a{i}") for i in range(3)]
        at_b = [sem(f"at_b{i}") for i in range(3)]
        in_done = [sem(f"in_done{i}") for i in range(2)]
        xc_ready = [sem(f"xc_ready{i}") for i in range(2)]
        sg_ready = [sem(f"sg_ready{i}") for i in range(2)]
        u0_ready = [sem(f"u0_ready{i}") for i in range(2)]
        bc_done = [sem(f"bc_done{i}") for i in range(2)]
        bm_ready = [sem(f"bm_ready{i}") for i in range(2)]
        bcp_ready = [sem(f"bcp_ready{i}") for i in range(2)]
        bc_ready = [sem(f"bc_ready{i}") for i in range(2)]
        dt_done = [sem(f"dt_done{i}") for i in range(2)]
        ex_ready = [sem(f"ex_ready{i}") for i in range(2)]
        exc_ready = [sem(f"exc_ready{i}") for i in range(2)]
        lg_ready = [sem(f"lg_ready{i}") for i in range(2)]
        dt_ready = [sem(f"dt_ready{i}") for i in range(2)]
        u1_ready = [sem(f"u1_ready{i}") for i in range(2)]
        o0_done = [sem(f"o0_done{i}") for i in range(2)]
        o1_done = [sem(f"o1_done{i}") for i in range(2)]
        zy_ready = [sem(f"zy_ready{i}") for i in range(2)]
        zb_ready = [sem(f"zb_ready{i}") for i in range(2)]
        z_ready = [sem(f"z_ready{i}") for i in range(2)]
        gate_done = sem("gate_done")
        lgt_ready = sem("lgt_ready")
        lsh_ready = sem("lsh_ready")
        lex_ready = sem("lex_ready")
        gate_step = sem("gate_step")
        cw_ready = sem("cw_ready")
        cwT_done = sem("cwT_done")
        cwT_ready = sem("cwT_ready")
        b2_done = sem("b2_done")
        acc_init = sem("acc_init")
        hid_done = sem("hid_done")
        gelu_done = sem("gelu_done")
        y_done = sem("y_done")
        py_ready = sem("py_ready")
        acc_add = sem("acc_add")

        def reuse(eng, last, n):
            if not isinstance(n, int) or n > 0:
                eng.wait_ge(last, n)

        def run_steps(eng, step, peeled=0):
            for t in range(4):
                step(t, *(t - k if t >= k else None for k in (1, 2, 3)))
            with eng.Fori(1, NCH - 3 - peeled) as i:
                step(i + 3, i + 2, i + 1, i)
            for t in range(NCH - peeled, NCH + 3):
                step(*(t - k if t - k < NCH else None for k in range(4)))

        block = ctx.enter_context(nc.Block())

        weight_loads = [
            (vrow[0:2 * NL, :], in_b.rearrange("l (h d) -> (l h) d", h=2)),
            (vrow[2 * NL:3 * NL, :], conv_w[:, conv_w.shape[1] - 1, :]),
            (vrow[3 * NL:4 * NL, :], conv_b),
            (vrow[4 * NL:5 * NL, :], dtproj_b),
            (vrow[5 * NL:6 * NL, :], D_param),
            (vrow[6 * NL:6 * NL + E, :], b1),
            (wr_s[:, :], w_real.rearrange("o i k -> o (i k)")),
            (wi_s[:, :], w_imag.rearrange("o i k -> o (i k)")),
            (ph[:, 0, :], phases.rearrange("(a k) -> a k", a=1).broadcast_to([COUT, K])),
            (ph[:, 1, :], phases.rearrange("(a k) -> a k", a=1).broadcast_to([COUT, K])),
            (xpw[:, :, :], xproj_w.rearrange("l d n -> d l n")),
            (dpw[:, :, :], dtproj_w.rearrange("l r d -> r l d")),
            (ow[:, :, :], out_w.rearrange("l d n -> d l n")),
            (w2s[:, :, :], W2.rearrange("e h d -> h e d")),
            (gbr[:, :], gate_b.rearrange("(a e) -> a e", a=1).broadcast_to([U, E])),
        ]
        for l in range(NL):
            weight_loads.append((obr[:, l, :], out_b[l:l + 1, :].broadcast_to([U, D])))
        for h in range(2):
            weight_loads.append((vrow[6 * NL + E:7 * NL + E, h * D:(h + 1) * D], ln_w))
            weight_loads.append((vrow[7 * NL + E:8 * NL + E, h * D:(h + 1) * D], ln_b))
            weight_loads.append((inw[h * D:(h + 1) * D, :, :], in_w.rearrange("l d n -> d l n")))
            weight_loads.append((gwf[h * D:(h + 1) * D, :], gate_w))
            weight_loads.append((w1f[h * D:(h + 1) * D, :, :], W1.rearrange("e d h -> d e h")))
        NW = 16 * (len(weight_loads) + NB)

        @block.sync
        def _(sp):
            for dst, src in weight_loads:
                sp.dma_start(dst, src).then_inc(s_w, 16)
            sp.wait_ge(s_pz, 1)
            for n in range(NB):
                sp.dma_start(b2d[n * EP:n * EP + E, n, :], b2).then_inc(s_w, 16)

            def load(c):
                reuse(sp, xt_ready, c)
                sp.dma_start(xs[:, :, :], xv[:, bass.ds(c * G, G), :]).then_inc(s_x, 16)

            def store(c):
                sp.wait_ge(acc_add, (c + 1) * E)
                sp.dma_start(out_pairs[:, bass.ds(c * G, G), :],
                             acc[0:U - 1, :].rearrange("u (g n) -> u g n", g=G)).then_inc(s_out, 16)
                sp.dma_start(out_last[:, bass.ds(c * G, G), :],
                             acc[U - 1:U, :].rearrange("u (g n) -> u g n", g=G)[:, :, 0:D]).then_inc(s_out, 16)

            def step(h, a, b, f):
                if h is not None and not (isinstance(h, int) and h == NCH - 1):
                    load(h + 1)
                if f is not None:
                    store(f)

            load(0)
            run_steps(sp, step, peeled=1)
            sp.wait_ge(s_out, 32 * NCH)

        @block.gpsimd
        def _(pool):
            pool.memset(b2d[:, :, :], 0.0).then_inc(s_pz, 1)
            pool.memset(cwt[:, :, :], 0.0).then_inc(s_pz, 1)
            pool.memset(nhalf[:, :], -0.5).then_inc(s_pz, 1)
            pool.memset(inv_d[:, :], 1.0 / D).then_inc(s_pz, 1)
            pool.memset(eps[:, :], EPS).then_inc(s_pz, 1)
            for e in range(E):
                pool.memset(rank[:, e:e + 1], float(E - e)).then_inc(s_pz, 1)
            pool.memset(ident[:, :], 0.0).then_inc(s_id, 1)
            pool.wait_ge(s_id, 1)
            pool.affine_select(out=ident[:, :], in_=ident[:, :], compare_op=ALU.not_equal, fill=1.0,
                               base=0, pattern=[[-1, 128]], channel_multiplier=1).then_inc(s_id, 1)
            pool.wait_ge(s_pz, 5 + E)
            pool.wait_ge(s_w, NW)

            def bcast(a):
                return a.rearrange("u (n a) -> u n a", a=1).broadcast_to([U, NB, D])

            def td(a):
                return a.rearrange("u (n d) -> u n d", d=D)

            def ln_rows(i, c):
                n = 1 if i else 7
                pool.wait_ge(ln_ve[i], c + 1)
                reuse(pool, ln_a[i], c)
                pool.tensor_tensor(lnr[:, i, :], lnve[:, i, :], nhalf[:, :], ALU.pow).then_inc(ln_small[i], 1)
                if i:
                    return
                pool.wait_ge(ln_small[i], c * n + 1)
                pool.tensor_tensor(r1q[:, :], lnr[:, i, :], lnr[:, i, :], ALU.mult).then_inc(ln_small[i], 1)
                pool.wait_ge(ln_small[i], c * n + 2)
                pool.tensor_tensor(r1v[:, :], r1q[:, :], lnvar[:, i, :], ALU.mult).then_inc(ln_small[i], 1)
                pool.wait_ge(ln_small[i], c * n + 3)
                pool.tensor_tensor(r1m[:, :], r1v[:, :], inv_d[:, :], ALU.mult).then_inc(ln_small[i], 1)
                pool.wait_ge(ln_small[i], c * n + 4)
                pool.tensor_tensor(r1w[:, :], r1m[:, :], eps[:, :], ALU.add).then_inc(ln_small[i], 1)
                pool.wait_ge(ln_small[i], c * n + 5)
                pool.tensor_tensor(r2[:, :], r1w[:, :], nhalf[:, :], ALU.pow).then_inc(ln_small[i], 1)
                pool.wait_ge(ln_small[i], c * n + 6)
                pool.tensor_tensor(r12[:, :], r2[:, :], lnr[:, i, :], ALU.mult).then_inc(ln_small[i], 1)

            def ln_split(i, c):
                pool.wait_ge(ln_small[i], (c + 1) * (1 if i else 7))
                reuse(pool, t2_done[i], 2 * c)
                reuse(pool, ln_lo[i], c)
                pool.tensor_tensor(lhl[:, i, :, 0:D].bitcast(F32R), td(lnd[:, i, :]),
                                   bcast(lnr[:, i, :] if i else r12[:, :]), ALU.mult).then_inc(ln_hi[i], 1)

            def base0(c):
                pool.wait_ge(ln_small[0], c * 7 + 1)
                reuse(pool, base_ready[0], c)
                pool.tensor_tensor(td(base_t[:, 0, :]), td(lnd[:, 0, :]), bcast(lnr[:, 0, :]), ALU.mult)\
                    .then_inc(base_part[0], 1)
                pool.wait_ge(base_part[0], c + 1)
                reuse(pool, zb_ready[0], c)
                pool.tensor_tensor(td(base[:, 0, :]), td(base_t[:, 0, :]),
                                   obr[:, 0:1, :].broadcast_to([U, NB, D]), ALU.add).then_inc(base_ready[0], 1)

            def base1_part(c):
                pool.wait_ge(c_saved, c + 1)
                reuse(pool, base_ready[1], c)
                pool.tensor_tensor(td(base_t[:, 1, :]), td(ct[:, :]), obr[:, 1:2, :].broadcast_to([U, NB, D]),
                                   ALU.add).then_inc(base_part[1], 1)

            def base1(c):
                pool.wait_ge(base_part[1], c + 1)
                pool.wait_ge(z_ready[0], c + 1)
                reuse(pool, zb_ready[1], c)
                pool.tensor_tensor(base[:, 1, :], base_t[:, 1, :], z[0][:, :], ALU.add).then_inc(base_ready[1], 1)

            def add_expert(e, c):
                pool.wait_ge(py_ready, c * E + e + 1)
                if e == 0:
                    pool.wait_ge(acc_init, c + 1)
                reuse(pool, acc_add, c * E + e)
                pool.tensor_tensor(acc[:, :], acc[:, :], py[e % 2][:, :], ALU.add).then_inc(acc_add, 1)

            def step(h, a, b, f):
                if a is not None:
                    base1_part(a)
                if a is not None:
                    ln_rows(1, a)
                    ln_split(1, a)
                if f is not None:
                    add_expert(0, f)
                    add_expert(1, f)
                if h is not None:
                    ln_rows(0, h)
                    ln_split(0, h)
                if f is not None:
                    add_expert(2, f)
                    add_expert(3, f)
                if b is not None:
                    ln_rows(2, b)
                    ln_split(2, b)
                if f is not None:
                    for e in range(4, E):
                        add_expert(e, f)
                if h is not None:
                    base0(h)
                if a is not None:
                    base1(a)

            run_steps(pool, step)

        @block.scalar
        def _(act):
            act.wait_ge(angles_ready, 1)
            act.activation(cs[:, :, :], phk[:, :, :], ACT.Sin).then_inc(sin_ready, 1)

            def head_hi(c):
                act.wait_ge(xt_ready, c + 1)
                reuse(act, conv_done, c)
                act.copy(xh[:, :, 0:UI], HEAD[:, 0:G * UI].rearrange("p (g v) -> p g v", g=G))\
                    .then_inc(xh_ready, 1)

            def head_conv(c):
                act.wait_ge(conv_done, c + 1)
                reuse(act, t1_done, c)
                act.copy(cf[:, :, :], HEAD[:, 0:G * U].rearrange("p (g u) -> p g u", g=G)).then_inc(cf_ready, 1)

            def head_tok(c):
                act.wait_ge(t1_done, c + 1)
                reuse(act, ln_d[0], c)
                reuse(act, base_part[1], c)
                act.copy(ct[:, :], HEAD[0:U, :]).then_inc(c_saved, 1)

            def ln_square(i, c):
                act.wait_ge(ln_d[i], c + 1)
                reuse(act, ln_var[i], c)
                act.activation(lnsq[:, i, :], lnd[:, i, :], ACT.Square).then_inc(ln_sq[i], 1)

            def at_second(i, c, src):
                act.wait_ge(t2_done[i], 2 * c + 2)
                if i < 2:
                    reuse(act, in_done[i], 4 * c)
                else:
                    reuse(act, hid_done, 2 * E * c)
                    reuse(act, gate_done, c)
                act.copy(at[i][:, HALF:2 * HALF], src[:, 0:HALF]).then_inc(at_b[i], 1)

            def silu_x(l, c):
                for h in range(2):
                    act.wait_ge(in_done[l], 4 * c + h + 1)
                    reuse(act, o0_done[l], c)
                    reuse(act, u0_ready[l], 2 * c)
                    act.activation(xc[l][:, h * HALF:(h + 1) * HALF], RING[l][h][:, 0:HALF], ACT.Silu,
                                   bias=bias_x[:, l:l + 1], scale=tapw[:, l:l + 1]).then_inc(xc_ready[l], 1)

            def silu_gate(l, c):
                for h in range(2):
                    act.wait_ge(in_done[l], 4 * c + h + 3)
                    act.activation(sg[l][:, h * HALF:(h + 1) * HALF], RING[l][h][:, 0:HALF], ACT.Silu,
                                   bias=bias_g[:, l:l + 1]).then_inc(sg_ready[l], 1)

            def states(l, c):
                for h in range(2):
                    act.wait_ge(bc_done[l], 2 * c + h + 1)
                    reuse(act, bcp_ready[l], 2 * c)
                    act.copy(bm[l][:, h * G:(h + 1) * G, :],
                             RING[l][h][0:U, :].rearrange("u (n s) -> u n s", n=G)[:, :, 0:DS])\
                        .then_inc(bm_ready[l], 1)

            def softplus_exp(l, c):
                for h in range(2):
                    act.wait_ge(dt_done[l], 2 * c + h + 1)
                    reuse(act, dt_ready[l], 2 * c)
                    act.activation(ex[l][:, h * HALF:(h + 1) * HALF], RING[l][h][:, 0:HALF], ACT.Exp,
                                   bias=dpb[:, l:l + 1]).then_inc(ex_ready[l], 1)

            def softplus_ln(l, c):
                for h in range(2):
                    act.wait_ge(exc_ready[l], 2 * c + h + 1)
                    act.activation(ex[l][:, h * HALF:(h + 1) * HALF], ex[l][:, h * HALF:(h + 1) * HALF],
                                   ACT.Ln, bias=1.0).then_inc(lg_ready[l], 1)

            def gate_exp(c):
                act.wait_ge(lsh_ready, c + 1)
                reuse(act, cw_ready, c)
                act.activation(lex[:, :, :], lsh[:, :, :], ACT.Exp).then_inc(lex_ready, 1)

            def gelu(e, c):
                for h in range(2):
                    act.wait_ge(hid_done, 2 * E * c + 2 * e + h + 1)
                    if e >= 2:
                        act.wait_ge(y_done, E * c + e - 1)
                    else:
                        reuse(act, y_done, E * c)
                    act.activation(gl[e % 2][:, h * HALF:(h + 1) * HALF], HID[h][:, 0:HALF], ACT.Gelu,
                                   bias=b1c[:, e:e + 1]).then_inc(gelu_done, 1)

            def step(h, a, b, f):
                if a is not None:
                    at_second(0, a, RING[0][1])
                if b is not None:
                    at_second(1, b, RING[1][1])
                if a is not None:
                    silu_x(0, a)
                if b is not None:
                    silu_x(1, b)
                if f is not None:
                    at_second(2, f, HID[1])
                if a is not None:
                    silu_gate(0, a)
                if b is not None:
                    silu_gate(1, b)
                act.preload_act_table_set("natural_log_exp_and_others")
                if f is not None:
                    gate_exp(f)
                if a is not None:
                    states(0, a)
                if b is not None:
                    states(1, b)
                if h is not None:
                    head_hi(h)
                if a is not None:
                    softplus_exp(0, a)
                if b is not None:
                    softplus_exp(1, b)
                if a is not None:
                    softplus_ln(0, a)
                if b is not None:
                    softplus_ln(1, b)
                if h is not None:
                    head_conv(h)
                    head_tok(h)
                if f is not None:
                    gelu(0, f)
                if a is not None:
                    ln_square(1, a)
                if f is not None:
                    gelu(1, f)
                if h is not None:
                    ln_square(0, h)
                if f is not None:
                    gelu(2, f)
                if b is not None:
                    ln_square(2, b)
                if f is not None:
                    for e in range(3, E):
                        gelu(e, f)

            act.wait_ge(weights_ready, 1)
            run_steps(act, step)

        @block.vector
        def _(dve):
            steps = [0]

            def link(ins):
                steps[0] += 1
                ins.then_inc(v_w, 1)
                dve.wait_ge(v_w, steps[0])

            dve.wait_ge(s_w, NW)
            dve.wait_ge(vcol_done, 1)
            dve.tensor_copy(vcol[:, :], bank[6][:, 0:NV]).then_inc(vcol_ready, 1)
            dve.wait_ge(vcol_ready, 1)
            link(dve.tensor_scalar(ph[:, 0, :], ph[:, 0, :], PI / 2, None, ALU.add))
            link(dve.tensor_scalar(cs[:, :, :], ph[:, :, :], 0.5 / PI, ROUND, ALU.mult, ALU.add))
            link(dve.tensor_scalar(cs[:, :, :], cs[:, :, :], -ROUND, None, ALU.add))
            link(dve.scalar_tensor_tensor(phk[:, :, :], cs[:, :, :], -TWO_PI_HI, ph[:, :, :], ALU.mult, ALU.add))
            link(dve.scalar_tensor_tensor(phk[:, :, :], cs[:, :, :], -TWO_PI_LO, phk[:, :, :], ALU.mult, ALU.add))
            dve.tensor_scalar(phk[:, :, :], phk[:, :, :], 3.1415925, -3.1415925, ALU.min, ALU.max)\
                .then_inc(angles_ready, 1)
            link(dve.memset(wk[:, :, :], 0.0))
            dve.memset(xh[:, :, UI:UI + 1].bitcast(F32), 0.0)
            dve.memset(xl[:, :, UI:UI + 1].bitcast(F32), 0.0)
            for l in range(NL):
                link(dve.tensor_scalar(inf[:, l, :], inw[:, l, :], lnw[:, l:l + 1], None, ALU.mult))
                link(dve.tensor_scalar(owd[:, l, :], ow[:, l, :], dpar[:, l:l + 1], None, ALU.mult))
            link(dve.tensor_copy(inh[:, :, :], inf[:, :, :]))
            dve.tensor_tensor(inl[:, :, :], inf[:, :, :], inh[:, :, :].bitcast(F32), ALU.subtract)
            link(dve.tensor_copy(w1h[:, :, :], w1f[:, :, :]))
            dve.tensor_tensor(w1l[:, :, :], w1f[:, :, :], w1h[:, :, :].bitcast(F32), ALU.subtract)
            link(dve.tensor_copy(gwh[:, :], gwf[:, :]))
            dve.tensor_tensor(gwl[:, :], gwf[:, :], gwh[:, :].bitcast(F32), ALU.subtract)
            dve.wait_ge(sin_ready, 1)

            def angle(n):
                return cs[:, n, :].rearrange("o (k a) -> o k a", a=1).broadcast_to([COUT, K, CIN])

            link(dve.tensor_tensor(wk[:, 1:K + 1, :], wr_s[:, :].rearrange("o (i k) -> o k i", k=K), angle(0), ALU.mult))
            link(dve.tensor_tensor(wk2[:, :, :], wi_s[:, :].rearrange("o (i k) -> o k i", k=K), angle(1), ALU.mult))
            dve.tensor_tensor(wk[:, 1:K + 1, :], wk[:, 1:K + 1, :], wk2[:, :, :], ALU.subtract).then_inc(wk_ready, 1)
            dve.wait_ge(xpT_done, 1)
            dve.tensor_copy(xpT[:, :, :], bank[4][0:RK, 0:NL * DI].rearrange("r (l d) -> r l d", l=NL))\
                .then_inc(xpT_ready, 1)
            dve.wait_ge(inbias_done, 1)
            link(dve.tensor_tensor(inb[:, :, :], inb[:, :, :],
                                   bank[3][:, 0:2 * NL].rearrange("d (l h) -> d l h", l=NL), ALU.add))
            link(dve.tensor_copy(bias_g[:, :], inb[:, :, 1]))
            link(dve.tensor_tensor(bias_s[:, :], inb[:, :, 0], tapw[:, :], ALU.mult))
            link(dve.tensor_tensor(bias_x[:, :], bias_s[:, :], tapb[:, :], ALU.add))
            dve.wait_ge(wdt_done, 1)
            link(dve.tensor_copy(wdt[:, :, :], bank[5][:, 0:NL * DI].rearrange("r (l d) -> r l d", l=NL)))
            dve.wait_ge(cwp_done, 1)
            for b in range(3):
                j0, j1 = 4 * b, min(4 * b + 4, JT)
                link(dve.tensor_copy(cwh[:, j0:j1, :],
                                     bank[b][:, 0:(j1 - j0) * 128].rearrange("p (j m) -> p j m", m=128)))
                link(dve.tensor_tensor(cwl[:, j0:j1, :],
                                       bank[b][:, 0:(j1 - j0) * 128].rearrange("p (j m) -> p j m", m=128),
                                       cwh[:, j0:j1, :].bitcast(F32), ALU.subtract))
            dve.nop().then_inc(weights_ready, 1)

            def td(a):
                return a.rearrange("u (n d) -> u n d", d=D)

            def bcast(a, w=D):
                return a.rearrange("u (n a) -> u n a", a=1).broadcast_to([U, NB, w])

            def head_lo(c):
                dve.wait_ge(xh_ready, c + 1)
                reuse(dve, conv_done, c)
                dve.tensor_tensor(xl[:, :, 0:UI], HEAD[:, 0:G * UI].rearrange("p (g v) -> p g v", g=G),
                                  xh[:, :, 0:UI].bitcast(F32), ALU.subtract).then_inc(xl_ready, 1)

            def ln_center(i, c, src):
                if i == 0:
                    dve.wait_ge(c_saved, c + 1)
                    reuse(dve, base_part[0], c)
                else:
                    dve.wait_ge(z_ready[i - 1], c + 1)
                reuse(dve, ln_d[i], c)
                dve.reduce_sum(lnsum[:, i, :], td(src[:, :]), AX.X).then_inc(ln_sum[i], 1)
                dve.wait_ge(ln_sum[i], c + 1)
                reuse(dve, ln_sq[i], c)
                reuse(dve, ln_a[i], c)
                reuse(dve, ln_hi[i], c)
                dve.scalar_tensor_tensor(td(lnd[:, i, :]), bcast(lnsum[:, i, :]), -1.0 / D, td(src[:, :]),
                                         ALU.mult, ALU.add).then_inc(ln_d[i], 1)

            def ln_variance(i, c):
                dve.wait_ge(ln_sq[i], c + 1)
                reuse(dve, ln_small[i], c * (1 if i else 7))
                reuse(dve, ln_ve[i], c)
                dve.reduce_sum(lnvar[:, i, :], td(lnsq[:, i, :]), AX.X).then_inc(ln_var[i], 1)
                dve.wait_ge(ln_var[i], c + 1)
                dve.tensor_scalar(lnve[:, i, :], lnvar[:, i, :], 1.0 / D, EPS, ALU.mult, ALU.add)\
                    .then_inc(ln_ve[i], 1)

            def ln_scale(i, c):
                dve.wait_ge(ln_small[i], (c + 1) * (1 if i else 7))
                reuse(dve, ln_lo[i], c)
                dve.tensor_tensor(td(lna[:, i, :]), td(lnd[:, i, :]), bcast(lnr[:, i, :] if i else r12[:, :]),
                                  ALU.mult).then_inc(ln_a[i], 1)

            def ln_split(i, c):
                dve.wait_ge(ln_hi[i], c + 1)
                dve.wait_ge(ln_a[i], c + 1)
                reuse(dve, t2_done[i], 2 * c)
                dve.tensor_tensor(lhl[:, i, :, D:2 * D], td(lna[:, i, :]), lhl[:, i, :, 0:D],
                                  ALU.subtract).then_inc(ln_lo[i], 1)

            def layernorm(i, c, src):
                ln_center(i, c, src)
                ln_variance(i, c)
                ln_scale(i, c)
                ln_split(i, c)

            def at_first(i, c, src):
                dve.wait_ge(t2_done[i], 2 * c + 1)
                if i < 2:
                    reuse(dve, in_done[i], 4 * c)
                else:
                    reuse(dve, hid_done, 2 * E * c)
                    reuse(dve, gate_done, c)
                dve.tensor_copy(at[i][:, 0:HALF], src[:, 0:HALF]).then_inc(at_a[i], 1)

            def gated(l, c):
                for h in range(2):
                    cols = slice(h * HALF, (h + 1) * HALF)
                    dve.wait_ge(xc_ready[l], 2 * c + h + 1)
                    dve.wait_ge(sg_ready[l], 2 * c + h + 1)
                    reuse(dve, o0_done[l], c)
                    reuse(dve, u1_ready[l], 2 * c)
                    dve.tensor_tensor(u0[l][:, cols], xc[l][:, cols], sg[l][:, cols], ALU.mult)\
                        .then_inc(u0_ready[l], 1)

            def states(l, c):
                for h in range(2):
                    dve.wait_ge(bm_ready[l], 2 * c + h + 1)
                    reuse(dve, bc_ready[l], c)
                    dve.tensor_tensor(bcp[l][:, h * G:(h + 1) * G, :],
                                      RING[l][h][0:U, :].rearrange("u (n s) -> u n s", n=G)[:, :, DS:2 * DS],
                                      bm[l][:, h * G:(h + 1) * G, :], ALU.mult).then_inc(bcp_ready[l], 1)
                dve.wait_ge(bcp_ready[l], 2 * c + 2)
                reuse(dve, zy_ready[l], c)
                dve.reduce_sum(bc[l][:, :], bcp[l][:, :, :], AX.X).then_inc(bc_ready[l], 1)

            def clamp(l, c):
                for h in range(2):
                    cols = slice(h * HALF, (h + 1) * HALF)
                    dve.wait_ge(ex_ready[l], 2 * c + h + 1)
                    dve.tensor_scalar(ex[l][:, cols], ex[l][:, cols], SOFTPLUS_CAP, None, ALU.min)\
                        .then_inc(exc_ready[l], 1)

            def steps_of_time(l, c):
                for h in range(2):
                    cols = slice(h * HALF, (h + 1) * HALF)
                    dve.wait_ge(lg_ready[l], 2 * c + h + 1)
                    reuse(dve, o1_done[l], c)
                    dve.scalar_tensor_tensor(dt[l][:, cols], RING[l][h][:, 0:HALF], dpb[:, l:l + 1], ex[l][:, cols],
                                             ALU.add, ALU.max).then_inc(dt_ready[l], 1)
                    dve.wait_ge(dt_ready[l], 2 * c + h + 1)
                    dve.wait_ge(u0_ready[l], 2 * c + h + 1)
                    dve.tensor_tensor(dt[l][:, cols], dt[l][:, cols], u0[l][:, cols], ALU.mult)\
                        .then_inc(u1_ready[l], 1)

            def layer_out(l, c):
                dve.wait_ge(o0_done[l], c + 1)
                dve.wait_ge(base_ready[l], c + 1)
                reuse(dve, z_ready[l], c)
                dve.tensor_tensor(zb[l][:, :], RING[l][0][0:U, :], base[:, l, :], ALU.add).then_inc(zb_ready[l], 1)
                dve.wait_ge(o1_done[l], c + 1)
                dve.wait_ge(bc_ready[l], c + 1)
                dve.tensor_tensor(td(zy[l][:, :]), td(RING[l][1][0:U, :]), bcast(bc[l][:, :]), ALU.mult)\
                    .then_inc(zy_ready[l], 1)
                dve.wait_ge(zb_ready[l], c + 1)
                dve.wait_ge(zy_ready[l], c + 1)
                reuse(dve, ln_d[l + 1], c)
                if l == 0:
                    reuse(dve, base_ready[1], c)
                else:
                    reuse(dve, acc_init, c)
                dve.tensor_tensor(z[l][:, :], zy[l][:, :], zb[l][:, :], ALU.add).then_inc(z_ready[l], 1)

            NGS = 15

            def gate(c):
                at_step = [0]

                def link(ins):
                    at_step[0] += 1
                    ins.then_inc(gate_step, 1)
                    dve.wait_ge(gate_step, c * NGS + at_step[0])

                def spread(a):
                    return bcast(a[:, :], E)

                ranks = rank[:, :].rearrange("u (a e) -> u a e", a=1).broadcast_to([U, NB, E])
                dve.wait_ge(gate_done, c + 1)
                link(dve.tensor_tensor(lgt[:, :, :], YB[0:U, 0:NB * E].rearrange("u (n e) -> u n e", e=E),
                                       gbr[:, :].rearrange("u (a e) -> u a e", a=1).broadcast_to([U, NB, E]), ALU.add))
                link(dve.reduce_max(lmx[:, :], lgt[:, :, :], AX.X))
                reuse(dve, lex_ready, c)
                dve.tensor_tensor(lsh[:, :, :], lgt[:, :, :], spread(lmx), ALU.subtract).then_inc(lsh_ready, 1)
                link(dve.tensor_tensor(leq[:, :, :], lgt[:, :, :], spread(lmx), ALU.is_equal))
                link(dve.tensor_tensor(lcd[:, :, :], leq[:, :, :], ranks, ALU.mult))
                link(dve.reduce_max(lkx[:, :], lcd[:, :, :], AX.X))
                link(dve.tensor_tensor(lhot[:, :, :], lcd[:, :, :], spread(lkx), ALU.is_equal))
                link(dve.scalar_tensor_tensor(lg2[:, :, :], lhot[:, :, :], LOGIT_DROP, lgt[:, :, :], ALU.mult, ALU.add))
                link(dve.reduce_max(lmx2[:, :], lg2[:, :, :], AX.X))
                link(dve.tensor_tensor(leq2[:, :, :], lg2[:, :, :], spread(lmx2), ALU.is_equal))
                link(dve.tensor_tensor(lcd2[:, :, :], leq2[:, :, :], ranks, ALU.mult))
                link(dve.reduce_max(lkx2[:, :], lcd2[:, :, :], AX.X))
                link(dve.tensor_tensor(lhot2[:, :, :], lcd2[:, :, :], spread(lkx2), ALU.is_equal))
                dve.tensor_tensor(lsel[:, :, :], lhot[:, :, :], lhot2[:, :, :], ALU.add)
                dve.wait_ge(lex_ready, c + 1)
                link(dve.reduce_sum(lsm[:, :], lex[:, :, :], AX.X))
                link(dve.reciprocal(lrc[:, :], lsm[:, :]))
                link(dve.tensor_tensor(lpw[:, :, :], lex[:, :, :], spread(lrc), ALU.mult))
                assert at_step[0] == NGS
                reuse(dve, py_ready, E * c)
                dve.tensor_tensor(cwt[:, :, 0:E], lpw[:, :, :], lsel[:, :, :], ALU.mult).then_inc(cw_ready, 1)

            def expert_base(c):
                dve.wait_ge(cwT_done, c + 1)
                reuse(dve, b2_done, c)
                dve.tensor_copy(cwT[:, :], YB[:, 0:U]).then_inc(cwT_ready, 1)

            def acc_start(c):
                dve.wait_ge(b2_done, c + 1)
                reuse(dve, s_out, 32 * c)
                dve.tensor_tensor(acc[:, :], YB[0:U, :], z[1][:, :], ALU.add).then_inc(acc_init, 1)

            def product(e, c):
                dve.wait_ge(y_done, c * E + e + 1)
                if e >= 2:
                    dve.wait_ge(acc_add, c * E + e - 1)
                else:
                    reuse(dve, acc_add, c * E)
                dve.tensor_tensor(td(py[e % 2][:, :]), td(YB[0:U, :]),
                                  cwt[:, :, e:e + 1].broadcast_to([U, NB, D]), ALU.mult).then_inc(py_ready, 1)

            def step(h, a, b, f):
                if a is not None:
                    at_first(0, a, RING[0][0])
                if b is not None:
                    at_first(1, b, RING[1][0])
                if f is not None:
                    at_first(2, f, HID[0])
                if a is not None:
                    gated(0, a)
                if f is not None:
                    gate(f)
                if b is not None:
                    gated(1, b)
                if a is not None:
                    states(0, a)
                if b is not None:
                    states(1, b)
                if h is not None:
                    head_lo(h)
                if f is not None:
                    expert_base(f)
                if a is not None:
                    clamp(0, a)
                if b is not None:
                    clamp(1, b)
                if a is not None:
                    steps_of_time(0, a)
                if b is not None:
                    steps_of_time(1, b)
                if f is not None:
                    acc_start(f)
                if a is not None:
                    layer_out(0, a)
                    ln_center(1, a, z[0])
                if b is not None:
                    layer_out(1, b)
                if f is not None:
                    product(0, f)
                if h is not None:
                    ln_center(0, h, ct)
                if a is not None:
                    ln_variance(1, a)
                if f is not None:
                    product(1, f)
                if b is not None:
                    ln_center(2, b, z[1])
                if h is not None:
                    ln_variance(0, h)
                if f is not None:
                    product(2, f)
                if a is not None:
                    ln_scale(1, a)
                    ln_split(1, a)
                if f is not None:
                    product(3, f)
                if b is not None:
                    ln_variance(2, b)
                if h is not None:
                    ln_scale(0, h)
                if f is not None:
                    product(4, f)
                if h is not None:
                    ln_split(0, h)
                if b is not None:
                    ln_scale(2, b)
                if f is not None:
                    product(5, f)
                if b is not None:
                    ln_split(2, b)
                if f is not None:
                    product(6, f)
                    product(7, f)

            run_steps(dve, step)

        @block.tensor
        def _(pe):
            pe.wait_ge(s_id, 2)
            pe.wait_ge(s_w, NW)
            pe.transpose(bank[6][:, 0:NV], vrow[:, :], ident[0:NV, 0:NV]).then_inc(vcol_done, 1)
            pe.wait_ge(vcol_ready, 1)
            for l in range(NL):
                for h in range(2):
                    mm = pe.matmul(bank[3][:, 2 * l + h:2 * l + h + 1], inw[0:D, l, h * DI:(h + 1) * DI],
                                   lnb[0:D, l:l + 1], start=True, stop=True)
            mm.then_inc(inbias_done, 1)
            for l in range(NL):
                mm = pe.transpose(bank[4][0:RK, l * DI:(l + 1) * DI], xpw[:, l, 0:RK], ident[:, :])
            mm.then_inc(xpT_done, 1)
            pe.wait_ge(xpT_ready, 1)
            for l in range(NL):
                mm = pe.matmul(bank[5][:, l * DI:(l + 1) * DI], xpT[:, l, :], dpw[:, l, :], start=True, stop=True)
            mm.then_inc(wdt_done, 1)
            pe.wait_ge(wk_ready, 1)
            for j in range(JT):
                for p in range(2):
                    mm = pe.transpose(bank[j // 4][:, (j % 4) * 128 + p * COUT:(j % 4) * 128 + (p + 1) * COUT],
                                      wk[:, 2 * j + 1 - p:2 * j + 3 - p, :].rearrange("o k i -> o (k i)"),
                                      ident[0:COUT, 0:COUT])
            mm.then_inc(cwp_done, 1)
            pe.wait_ge(weights_ready, 1)

            def cols(n):
                return slice(n * U, (n + 1) * U)

            def transpose_x(c):
                pe.wait_ge(s_x, 16 * (c + 1))
                reuse(pe, c_saved, c)
                for g in range(G):
                    mm = pe.transpose(HEAD[:, g * UI:(g + 1) * UI], xs[:, g, :], ident[0:UI, 0:UI])
                mm.then_inc(xt_ready, 1)

            def conv(c):
                pe.wait_ge(xl_ready, c + 1)
                n = 0
                for w, v in ((cwh, xh), (cwh, xl), (cwl, xh)):
                    for j in range(JT):
                        mm = pe.matmul(HEAD[:, 0:G * U], w[:, j, :], v[:, :, j:j + U],
                                       start=(n == 0), stop=(n == 3 * JT - 1))
                        n += 1
                mm.then_inc(conv_done, 1)

            def transpose_c(c):
                pe.wait_ge(cf_ready, c + 1)
                for g in range(G):
                    mm = pe.transpose(HEAD[0:U, g * 128:(g + 1) * 128], cf[:, g, :], ident[:, :])
                mm.then_inc(t1_done, 1)

            def transpose_rows(i, c, to):
                pe.wait_ge(ln_lo[i], c + 1)
                for h in range(2):
                    if i < 2:
                        reuse(pe, [zb_ready, zy_ready][h][i], c)
                    else:
                        reuse(pe, gelu_done, 2 * E * c)
                    for n in range(G):
                        mm = pe.transpose(to[h][:, cols(n)], lhl[:, i, h * G + n, :], ident[0:U, 0:U])
                    mm.then_inc(t2_done[i], 1)

            def project_in(l, m, c):
                for h in range(2):
                    if m:
                        pe.wait_ge(xc_ready[l], 2 * c + h + 1)
                    else:
                        pe.wait_ge([at_a, at_b][h][l], c + 1)
                    for n, w in enumerate((inh, inl)):
                        mm = pe.matmul(RING[l][h][:, 0:HALF], w[:, l, m * DI:(m + 1) * DI],
                                       at[l][:, h * HALF:(h + 1) * HALF], start=(n == 0), stop=(n == 1))
                    mm.then_inc(in_done[l], 1)

            def project_states(l, c):
                pe.wait_ge(xc_ready[l], 2 * c + 2)
                for h in range(2):
                    pe.wait_ge(sg_ready[l], 2 * c + h + 1)
                    for n in range(G):
                        mm = pe.matmul(RING[l][h][0:U, n * 128:(n + 1) * 128], xc[l][:, cols(h * G + n)],
                                       xpw[:, l, RK:RK + 2 * DS], start=True, stop=True)
                    mm.then_inc(bc_done[l], 1)

            def project_dt(l, c):
                for h in range(2):
                    pe.wait_ge(bcp_ready[l], 2 * c + h + 1)
                    pe.matmul(RING[l][h][:, 0:HALF], wdt[:, l, :], xc[l][:, h * HALF:(h + 1) * HALF],
                              start=True, stop=True).then_inc(dt_done[l], 1)

            def project_out0(l, c):
                pe.wait_ge(dt_ready[l], 2 * c + 1)
                pe.wait_ge(u0_ready[l], 2 * c + 2)
                for n in range(NB):
                    mm = pe.matmul(RING[l][0][0:U, n * D:(n + 1) * D], u0[l][:, cols(n)], owd[:, l, :],
                                   start=True, stop=True)
                mm.then_inc(o0_done[l], 1)

            def project_out1(l, c):
                pe.wait_ge(u1_ready[l], 2 * c + 2)
                for n in range(NB):
                    mm = pe.matmul(RING[l][1][0:U, n * D:(n + 1) * D], dt[l][:, cols(n)], ow[:, l, :],
                                   start=True, stop=True)
                mm.then_inc(o1_done[l], 1)

            def gate(c):
                pe.wait_ge(at_a[2], c + 1)
                pe.wait_ge(at_b[2], c + 1)
                reuse(pe, py_ready, E * c)
                for n in range(NB):
                    for k, w in enumerate((gwh, gwl)):
                        mm = pe.matmul(YB[0:U, n * E:(n + 1) * E], at[2][:, cols(n)], w[:, :],
                                       start=(k == 0), stop=(k == 1))
                mm.then_inc(gate_done, 1)

            def expert_weights(c):
                pe.wait_ge(cw_ready, c + 1)
                pe.transpose(YB[:, 0:U], cwt[:, :, :].rearrange("u n e -> u (n e)"), ident[0:U, 0:U])\
                    .then_inc(cwT_done, 1)

            def expert_bias(c):
                pe.wait_ge(cwT_ready, c + 1)
                pe.matmul(YB[0:U, :], cwT[:, :], b2d[:, :, :].rearrange("k n d -> k (n d)"),
                          start=True, stop=True).then_inc(b2_done, 1)

            def hidden(e, c):
                for h in range(2):
                    if e:
                        pe.wait_ge(gelu_done, 2 * E * c + 2 * e + h - 1)
                    for k, w in enumerate((w1h, w1l)):
                        mm = pe.matmul(HID[h][:, 0:HALF], w[:, e, :], at[2][:, h * HALF:(h + 1) * HALF],
                                       start=(k == 0), stop=(k == 1))
                    mm.then_inc(hid_done, 1)

            def expert_out(e, c):
                if e:
                    pe.wait_ge(py_ready, E * c + e)
                else:
                    pe.wait_ge(acc_init, c + 1)
                pe.wait_ge(gelu_done, 2 * E * c + 2 * e + 2)
                for n in range(NB):
                    mm = pe.matmul(YB[0:U, n * D:(n + 1) * D], gl[e % 2][:, cols(n)], w2s[:, e, :],
                                   start=True, stop=True)
                mm.then_inc(y_done, 1)

            def step(h, a, b, f):
                if a is not None:
                    transpose_rows(0, a, RING[0])
                if b is not None:
                    transpose_rows(1, b, RING[1])
                if a is not None:
                    project_in(0, 0, a)
                if b is not None:
                    project_in(1, 0, b)
                if f is not None:
                    transpose_rows(2, f, HID)
                if a is not None:
                    project_in(0, 1, a)
                if b is not None:
                    project_in(1, 1, b)
                if f is not None:
                    gate(f)
                if a is not None:
                    project_states(0, a)
                if b is not None:
                    project_states(1, b)
                if h is not None:
                    transpose_x(h)
                if a is not None:
                    project_dt(0, a)
                if b is not None:
                    project_dt(1, b)
                if f is not None:
                    expert_weights(f)
                if h is not None:
                    conv(h)
                if f is not None:
                    expert_bias(f)
                    hidden(0, f)
                if h is not None:
                    transpose_c(h)
                if a is not None:
                    project_out0(0, a)
                if b is not None:
                    project_out0(1, b)
                if a is not None:
                    project_out1(0, a)
                if b is not None:
                    project_out1(1, b)
                if f is not None:
                    for e in range(E):
                        if e + 1 < E:
                            hidden(e + 1, f)
                        expert_out(e, f)

            run_steps(pe, step)


_INS = ['x', 'L0_tok_w_real', 'L0_tok_w_imag', 'L0_tok_phases', 'L0_attn_ln_w', 'L0_attn_ln_b', 'L0_attn_in_w',
        'L0_attn_in_b', 'L0_attn_conv_w', 'L0_attn_conv_b', 'L0_attn_xproj_w', 'L0_attn_dtproj_w',
        'L0_attn_dtproj_b', 'L0_attn_D_param', 'L0_attn_out_w', 'L0_attn_out_b', 'L0_ffn_gate_w',
        'L0_ffn_gate_b', 'L0_ffn_W1', 'L0_ffn_b1', 'L0_ffn_W2', 'L0_ffn_b2']
_OUTS = [((64, 235, 64), 'float32')]


def kernel(**inputs):
    import numpy as _np
    import concourse.bacc as _bacc
    from concourse import mybir as _mybir
    from concourse.bass_utils import run_bass_kernel_spmd as _run

    nc = _bacc.Bacc("TRN2", target_bir_lowering=False, num_devices=1)
    arrays, args = {}, []
    for name in _INS:
        a = _np.ascontiguousarray(inputs[name])
        arrays[f"in_{name}_dram"] = a
        args.append(nc.dram_tensor(f"in_{name}_dram", a.shape, _mybir.dt.from_np(a.dtype), kind="ExternalInput").ap())
    for i, (shape, dtype) in enumerate(_OUTS):
        dt = _mybir.dt.from_np(_np.dtype(dtype))
        args.append(nc.dram_tensor(f"out_{i}_dram", shape, dt, kind="ExternalOutput").ap())
    audio_tower(nc, *args)
    r = _run(nc, [arrays], core_ids=[0])
    got = tuple(r.results[0][f"out_{i}_dram"] for i in range(len(_OUTS)))
    return got[0]
```

```python
from contextlib import ExitStack

import concourse.bass as bass
from concourse import mybir

ALU = mybir.AluOpType
ACT = mybir.ActivationFunctionType
AX = mybir.AxisListType
F32 = mybir.dt.float32
F32R = mybir.dt.float32r

EPS = 1e-5
PI = 3.14159265358979
ROUND = 12582912.0
TWO_PI_HI = 6.28125
TWO_PI_LO = 1.9353071795864769e-3
SOFTPLUS_CAP = 1e18
LOGIT_DROP = -3.0e38


def audio_tower(nc, x, w_real, w_imag, phases, ln_w, ln_b, in_w, in_b, conv_w, conv_b, xproj_w,
                dtproj_w, dtproj_b, D_param, out_w, out_b, gate_w, gate_b, W1, b1, W2, b2, out):
    B, S, CIN = x.shape
    COUT, _, K = w_real.shape
    SO = S - K + 1
    NL, D, DI2 = in_w.shape
    DI = DI2 // 2
    DS = (xproj_w.shape[2] - dtproj_w.shape[1]) // 2
    RK = dtproj_w.shape[1]
    E, _, H = W1.shape
    G = 4
    NCH = B // G
    UI = S // 2
    U = (SO + 1) // 2
    JT = K // 2 + 1
    NB = 2 * G
    HALF = NB // 2 * U
    TD = NB * D
    EP = 128 // NB

    xv = x.rearrange("b (v c) i -> v b (c i)", c=2)
    out_pairs = out[:, 0:2 * (U - 1), :].rearrange("b (u c) d -> u b (c d)", c=2)
    out_last = out[:, 2 * (U - 1):SO, :].rearrange("b c d -> c b d")

    with ExitStack() as ctx:
        def sb(name, shape, dt=F32):
            return ctx.enter_context(nc.sbuf_tensor(name, shape, dt))

        def sem(name):
            return ctx.enter_context(nc.semaphore(name))

        bank = [ctx.enter_context(nc.psum_tensor(f"bank{i}", [128, 512], F32)) for i in range(8)]
        HEAD = bank[0]
        RING = [[bank[1], bank[2]], [bank[3], bank[4]]]
        HID = [bank[5], bank[6]]
        YB = bank[7]
        YBANK = [YB, HEAD]

        ident = sb("ident", [128, 128])
        NV = 8 * NL + E
        vrow = sb("vrow", [NV, 128])
        vcol = sb("vcol", [128, NV])
        inb = vcol[:, 0:2 * NL].rearrange("d (l h) -> d l h", l=NL)
        tapw, tapb, dpb, dpar = (vcol[:, (2 + i) * NL:(3 + i) * NL] for i in range(4))
        b1c = vcol[:, 6 * NL:6 * NL + E]
        lnw, lnb = (vcol[:, 6 * NL + E + i * NL:6 * NL + E + (i + 1) * NL] for i in range(2))
        wr_s = sb("wr_s", [COUT, CIN * K])
        wi_s = sb("wi_s", [COUT, CIN * K])
        ph = sb("ph", [COUT, 2, K])
        phk = sb("phk", [COUT, 2, K])
        cs = sb("cs", [COUT, 2, K])
        wk = sb("wk", [COUT, K + 3, CIN])
        wk2 = sb("wk2", [COUT, K, CIN])
        cwf = sb("cwf", [128, JT, 128])
        cwh = sb("cwh", [128, JT, 128], F32R)
        cwl = sb("cwl", [128, JT, 128], F32R)
        inw = sb("inw", [128, NL, DI2])
        inf = sb("inf", [128, NL, DI2])
        inh = sb("inh", [128, NL, DI2], F32R)
        inl = sb("inl", [128, NL, DI2], F32R)
        bias_g = sb("bias_g", [DI, NL])
        bias_s = sb("bias_s", [DI, NL])
        bias_x = sb("bias_x", [DI, NL])
        xpw = sb("xpw", [DI, NL, RK + 2 * DS])
        xpT = sb("xpT", [RK, NL, DI])
        dpw = sb("dpw", [RK, NL, DI])
        wdt = sb("wdt", [DI, NL, DI])
        ow = sb("ow", [DI, NL, D])
        obr = sb("obr", [U, NL, D])
        gwf = sb("gwf", [128, E])
        gw2 = sb("gw2", [128, 2, E], F32R)
        gbr = sb("gbr", [U, E])
        rank = sb("rank", [U, E])
        w1f = sb("w1f", [128, E, H])
        w1h = sb("w1h", [128, E, H], F32R)
        w1l = sb("w1l", [128, E, H], F32R)
        w2s = sb("w2s", [H, E, D])
        b2d = sb("b2d", [128, NB, D])
        nhalf = sb("nhalf", [U, 2, NB])

        NPY = 4
        OUTER = 3
        xs = sb("xs", [UI, G, 128])
        xh = sb("xh", [128, G, UI + 1], F32R)
        xl = sb("xl", [128, G, UI + 1], F32R)
        cf = sb("cf", [128, G, U])
        ct = sb("ct", [U, TD])
        lnsum = sb("lnsum", [U, 3, NB])
        lnd = sb("lnd", [U, 3, TD])
        lnsq = sb("lnsq", [U, 3, TD])
        lnvar = sb("lnvar", [U, 3, NB])
        lnve = sb("lnve", [U, 4, NB])
        lnr = sb("lnr", [U, 4, NB])
        lna = sb("lna", [U, 3, TD])
        lhl = sb("lhl", [U, 3, NB, 2 * D])
        base = sb("base", [U, 2, TD])
        base_t = sb("base_t", [U, 2, TD])
        at = [sb(f"at{i}", [128, 2 * HALF], F32R) for i in range(3)]
        xc = [sb(f"xc{i}", [DI, 2 * HALF]) for i in range(2)]
        sg = [sb(f"sg{i}", [DI, 2 * HALF]) for i in range(2)]
        u0 = [sb(f"u0{i}", [DI, 2 * HALF]) for i in range(2)]
        ex = [sb(f"ex{i}", [DI, 2 * HALF]) for i in range(2)]
        dt = [sb(f"dt{i}", [DI, 2 * HALF]) for i in range(2)]
        bm = [sb(f"bm{i}", [U, NB, DS]) for i in range(2)]
        bcp = [sb(f"bcp{i}", [U, NB, DS]) for i in range(2)]
        bc = [sb(f"bc{i}", [U, NB]) for i in range(2)]
        z = [sb(f"z{i}", [U, TD]) for i in range(2)]
        lgh = sb("lgh", [U, NB, E])
        lgt = sb("lgt", [U, NB, E])
        lmx = sb("lmx", [U, NB])
        lcd = sb("lcd", [U, NB, E])
        lkx = sb("lkx", [U, NB])
        lhot = sb("lhot", [U, NB, E])
        lg2 = sb("lg2", [U, NB, E])
        lmx2 = sb("lmx2", [U, NB])
        leq2 = sb("leq2", [U, NB, E])
        lcd2 = sb("lcd2", [U, NB, E])
        lkx2 = sb("lkx2", [U, NB])
        lhot2 = sb("lhot2", [U, NB, E])
        lsel = sb("lsel", [U, NB, E])
        lsh = sb("lsh", [U, NB, E])
        lex = sb("lex", [U, NB, E])
        lsm = sb("lsm", [U, NB])
        lrc = sb("lrc", [U, NB])
        lpw = sb("lpw", [U, NB, E])
        cwt = sb("cwt", [U, NB, EP])
        cwT = sb("cwT", [128, U])
        gl = [sb(f"gl{i}", [H, 2 * HALF]) for i in range(2)]
        py = [sb(f"py{i}", [U, TD]) for i in range(NPY)]
        acc = sb("acc", [U, TD])

        s_w = sem("weights_in")
        s_id = sem("ident_ready")
        s_pz = sem("pool_consts")
        v_w = sem("dve_weight_step")
        angles_ready = sem("angles_ready")
        sin_ready = sem("sin_ready")
        vcol_done = sem("vcol_done")
        vcol_ready = sem("vcol_ready")
        wk_ready = sem("wk_ready")
        cwp_done = sem("cwp_done")
        xpT_done = sem("xpT_done")
        xpT_ready = sem("xpT_ready")
        inbias_done = sem("inbias_done")
        wdt_done = sem("wdt_done")
        weights_ready = sem("weights_ready")
        s_x = sem("x_in")
        s_out = sem("out_stored")
        xt_ready = sem("xt_ready")
        xh_ready = sem("xh_ready")
        xl_ready = sem("xl_ready")
        conv_done = sem("conv_done")
        cf_ready = sem("cf_ready")
        t1_done = sem("t1_done")
        c_saved = sem("c_saved")
        ln_sum = [sem(f"ln_sum{i}") for i in range(3)]
        ln_d = [sem(f"ln_d{i}") for i in range(3)]
        ln_sq = [sem(f"ln_sq{i}") for i in range(3)]
        ln_ve = [sem(f"ln_ve{i}") for i in range(3)]
        ln_var = [sem(f"ln_var{i}") for i in range(3)]
        ln_r = [sem(f"ln_r{i}") for i in range(3)]
        ln_a = [sem(f"ln_a{i}") for i in range(3)]
        ln_hi = [sem(f"ln_hi{i}") for i in range(3)]
        ln_lo = [sem(f"ln_lo{i}") for i in range(3)]
        base_part = [sem(f"base_part{i}") for i in range(2)]
        base_ready = [sem(f"base_ready{i}") for i in range(2)]
        t2_done = [sem(f"t2_done{i}") for i in range(3)]
        at_a = [sem(f"at_a{i}") for i in range(3)]
        at_b = [sem(f"at_b{i}") for i in range(3)]
        in_done = [sem(f"in_done{i}") for i in range(2)]
        xc_ready = [sem(f"xc_ready{i}") for i in range(2)]
        sg_ready = [sem(f"sg_ready{i}") for i in range(2)]
        u0_ready = [sem(f"u0_ready{i}") for i in range(2)]
        bc_done = [sem(f"bc_done{i}") for i in range(2)]
        bm_ready = [sem(f"bm_ready{i}") for i in range(2)]
        bcp_ready = [sem(f"bcp_ready{i}") for i in range(2)]
        bc_ready = [sem(f"bc_ready{i}") for i in range(2)]
        dt_done = [sem(f"dt_done{i}") for i in range(2)]
        ex_ready = [sem(f"ex_ready{i}") for i in range(2)]
        exc_ready = [sem(f"exc_ready{i}") for i in range(2)]
        lg_ready = [sem(f"lg_ready{i}") for i in range(2)]
        dt_ready = [sem(f"dt_ready{i}") for i in range(2)]
        spread_done = [sem(f"spread_done{i}") for i in range(2)]
        dbc_ready = [sem(f"dbc_ready{i}") for i in range(2)]
        u1_ready = [sem(f"u1_ready{i}") for i in range(2)]
        o_done = [sem(f"o_done{i}") for i in range(2)]
        z_ready = [sem(f"z_ready{i}") for i in range(2)]
        gate_done = sem("gate_done")
        lgt_ready = sem("lgt_ready")
        lsh_ready = sem("lsh_ready")
        lex_ready = sem("lex_ready")
        gate_step = sem("gate_step")
        gate_end = sem("gate_end")
        cw_ready = sem("cw_ready")
        cwT_done = sem("cwT_done")
        cwT_ready = sem("cwT_ready")
        b2_done = sem("b2_done")
        acc_init = sem("acc_init")
        hid_done = sem("hid_done")
        gelu_done = sem("gelu_done")
        y_done = sem("y_done")
        py_ready = sem("py_ready")
        acc_add = sem("acc_add")

        def reuse(eng, last, n):
            if not isinstance(n, int) or n > 0:
                eng.wait_ge(last, n)

        def on(c, stage, *which):
            if c is not None:
                stage(*which, c)

        def src_of(i):
            return RING[i] if i < 2 else HID

        def run_steps(eng, step, peeled=0):
            for t in range(4):
                step(t, *(t - k if t >= k else None for k in (1, 2, 3)))
            with eng.Fori(1, NCH - 3 - peeled) as i:
                step(i + 3, i + 2, i + 1, i)
            for t in range(NCH - peeled, NCH + 3):
                step(*(t - k if t - k < NCH else None for k in range(4)))

        block = ctx.enter_context(nc.Block())

        weight_loads = [
            (vrow[0:2 * NL, :], in_b.rearrange("l (h d) -> (l h) d", h=2)),
            (vrow[2 * NL:3 * NL, :], conv_w[:, conv_w.shape[1] - 1, :]),
            (vrow[3 * NL:4 * NL, :], conv_b),
            (vrow[4 * NL:5 * NL, :], dtproj_b),
            (vrow[5 * NL:6 * NL, :], D_param),
            (vrow[6 * NL:6 * NL + E, :], b1),
            (wr_s[:, :], w_real.rearrange("o i k -> o (i k)")),
            (wi_s[:, :], w_imag.rearrange("o i k -> o (i k)")),
            (ph[:, 0, :], phases.rearrange("(a k) -> a k", a=1).broadcast_to([COUT, K])),
            (ph[:, 1, :], phases.rearrange("(a k) -> a k", a=1).broadcast_to([COUT, K])),
            (xpw[:, :, :], xproj_w.rearrange("l d n -> d l n")),
            (dpw[:, :, :], dtproj_w.rearrange("l r d -> r l d")),
            (ow[:, :, :], out_w.rearrange("l d n -> d l n")),
            (w2s[:, :, :], W2.rearrange("e h d -> h e d")),
            (gbr[:, :], gate_b.rearrange("(a e) -> a e", a=1).broadcast_to([U, E])),
        ]
        for l in range(NL):
            weight_loads.append((obr[:, l, :], out_b[l:l + 1, :].broadcast_to([U, D])))
        for h in range(2):
            weight_loads.append((vrow[6 * NL + E:7 * NL + E, h * D:(h + 1) * D], ln_w))
            weight_loads.append((vrow[7 * NL + E:8 * NL + E, h * D:(h + 1) * D], ln_b))
            weight_loads.append((inw[h * D:(h + 1) * D, :, :], in_w.rearrange("l d n -> d l n")))
            weight_loads.append((gwf[h * D:(h + 1) * D, :], gate_w))
            weight_loads.append((w1f[h * D:(h + 1) * D, :, :], W1.rearrange("e d h -> d e h")))
        NW = 16 * (len(weight_loads) + NB)

        @block.sync
        def _(sp):
            for dst, src in weight_loads:
                sp.dma_start(dst, src).then_inc(s_w, 16)
            sp.wait_ge(s_pz, 1)
            for n in range(NB):
                sp.dma_start(b2d[n * EP:n * EP + E, n, :], b2).then_inc(s_w, 16)

            def load(c):
                reuse(sp, xt_ready, c)
                sp.dma_start(xs[:, :, :], xv[:, bass.ds(c * G, G), :]).then_inc(s_x, 16)

            def store(c):
                sp.wait_ge(acc_add, (c + 1) * E)
                sp.dma_start(out_pairs[:, bass.ds(c * G, G), :],
                             acc[0:U - 1, :].rearrange("u (g n) -> u g n", g=G)).then_inc(s_out, 16)
                sp.dma_start(out_last[:, bass.ds(c * G, G), :],
                             acc[U - 1:U, :].rearrange("u (g n) -> u g n", g=G)[:, :, 0:D]).then_inc(s_out, 16)

            def step(h, a, b, f):
                if h is not None and not (isinstance(h, int) and h == NCH - 1):
                    load(h + 1)
                if f is not None:
                    store(f)

            load(0)
            run_steps(sp, step, peeled=1)
            sp.wait_ge(s_out, 32 * NCH)

        @block.gpsimd
        def _(pool):
            pool.memset(b2d[:, :, :], 0.0).then_inc(s_pz, 1)
            pool.memset(cwt[:, :, :], 0.0).then_inc(s_pz, 1)
            pool.memset(nhalf[:, :, :], -0.5).then_inc(s_pz, 1)
            for e in range(E):
                pool.memset(rank[:, e:e + 1], float(E - e)).then_inc(s_pz, 1)
            pool.memset(ident[:, :], 0.0).then_inc(s_id, 1)
            pool.wait_ge(s_id, 1)
            pool.affine_select(out=ident[:, :], in_=ident[:, :], compare_op=ALU.not_equal, fill=1.0,
                               base=0, pattern=[[-1, 128]], channel_multiplier=1).then_inc(s_id, 1)
            pool.wait_ge(s_pz, 3 + E)
            pool.wait_ge(s_w, NW)

            def bcast(a):
                return a.rearrange("u (n a) -> u n a", a=1).broadcast_to([U, NB, D])

            def td(a):
                return a.rearrange("u (n d) -> u n d", d=D)

            def ln_rows(i, c):
                slots = slice(i, i + 1) if i else slice(0, OUTER + 1, OUTER)
                n = 1 if i else 2
                pool.wait_ge(ln_ve[i], c + 1)
                reuse(pool, ln_a[i], c)
                if i == 0:
                    reuse(pool, base_part[0], c)
                pool.tensor_tensor(lnr[:, slots, :], lnve[:, slots, :], nhalf[:, 0:n, :], ALU.pow).then_inc(ln_r[i], 1)

            def ln_split(i, c):
                pool.wait_ge(ln_r[i], c + 1)
                reuse(pool, t2_done[i], 2 * c)
                reuse(pool, ln_lo[i], c)
                pool.tensor_tensor(lhl[:, i, :, 0:D].bitcast(F32R), td(lnd[:, i, :]),
                                   bcast(lnr[:, i, :]), ALU.mult).then_inc(ln_hi[i], 1)

            def base0(c):
                pool.wait_ge(ln_r[0], c + 1)
                reuse(pool, base_ready[0], c)
                pool.tensor_tensor(td(base_t[:, 0, :]), td(lnd[:, 0, :]), bcast(lnr[:, OUTER, :]), ALU.mult)\
                    .then_inc(base_part[0], 1)
                pool.wait_ge(base_part[0], c + 1)
                reuse(pool, z_ready[0], c)
                pool.tensor_tensor(td(base[:, 0, :]), td(base_t[:, 0, :]),
                                   obr[:, 0:1, :].broadcast_to([U, NB, D]), ALU.add).then_inc(base_ready[0], 1)

            def base1_part(c):
                pool.wait_ge(c_saved, c + 1)
                reuse(pool, base_ready[1], c)
                pool.tensor_tensor(td(base_t[:, 1, :]), td(ct[:, :]), obr[:, 1:2, :].broadcast_to([U, NB, D]),
                                   ALU.add).then_inc(base_part[1], 1)

            def base1(c):
                pool.wait_ge(base_part[1], c + 1)
                pool.wait_ge(z_ready[0], c + 1)
                reuse(pool, z_ready[1], c)
                pool.tensor_tensor(base[:, 1, :], base_t[:, 1, :], z[0][:, :], ALU.add).then_inc(base_ready[1], 1)

            def gated(l, c):
                for h in range(2):
                    cols = slice(h * HALF, (h + 1) * HALF)
                    pool.wait_ge(xc_ready[l], 2 * c + h + 1)
                    pool.wait_ge(sg_ready[l], 2 * c + h + 1)
                    reuse(pool, u1_ready[l], 2 * c)
                    pool.tensor_tensor(u0[l][:, cols], xc[l][:, cols], sg[l][:, cols], ALU.mult)\
                        .then_inc(u0_ready[l], 1)

            def add_expert(e, c):
                pool.wait_ge(py_ready, c * E + e + 1)
                if e == 0:
                    pool.wait_ge(acc_init, c + 1)
                reuse(pool, acc_add, c * E + e)
                pool.tensor_tensor(acc[:, :], acc[:, :], py[e % NPY][:, :], ALU.add).then_inc(acc_add, 1)

            def step(h, a, b, f):
                on(a, gated, 0)
                on(b, gated, 1)
                on(b, base1)
                on(a, base0)
                on(a, base1_part)
                on(h, ln_rows, 0)
                on(h, ln_split, 0)
                on(a, ln_rows, 1)
                on(f, add_expert, 0)
                on(a, ln_split, 1)
                on(f, add_expert, 1)
                on(b, ln_rows, 2)
                on(f, add_expert, 2)
                on(b, ln_split, 2)
                for e in range(3, E):
                    on(f, add_expert, e)

            run_steps(pool, step)

        @block.scalar
        def _(act):
            act.wait_ge(angles_ready, 1)
            act.activation(cs[:, :, :], phk[:, :, :], ACT.Sin).then_inc(sin_ready, 1)

            def head_hi(c):
                act.wait_ge(xt_ready, c + 1)
                reuse(act, conv_done, c)
                act.copy(xh[:, :, 0:UI], HEAD[:, 0:G * UI].rearrange("p (g v) -> p g v", g=G))\
                    .then_inc(xh_ready, 1)

            def head_conv(c):
                act.wait_ge(conv_done, c + 1)
                reuse(act, t1_done, c)
                act.copy(cf[:, :, :], HEAD[:, 0:G * U].rearrange("p (g u) -> p g u", g=G)).then_inc(cf_ready, 1)

            def head_tok(c):
                act.wait_ge(t1_done, c + 1)
                reuse(act, ln_d[0], c)
                reuse(act, base_part[1], c)
                act.copy(ct[:, :], HEAD[0:U, :]).then_inc(c_saved, 1)

            def ln_square(i, c):
                act.wait_ge(ln_d[i], c + 1)
                reuse(act, ln_var[i], c)
                act.activation(lnsq[:, i, :], lnd[:, i, :], ACT.Square).then_inc(ln_sq[i], 1)

            def at_second(i, c):
                act.wait_ge(t2_done[i], 2 * c + 2)
                if i < 2:
                    reuse(act, in_done[i], 4 * c)
                else:
                    reuse(act, hid_done, 2 * E * c)
                    reuse(act, gate_done, c)
                act.copy(at[i][:, HALF:2 * HALF], src_of(i)[1][:, 0:HALF]).then_inc(at_b[i], 1)

            def silu_x(l, c):
                for h in range(2):
                    act.wait_ge(in_done[l], 4 * c + h + 1)
                    reuse(act, dt_done[l], 2 * c)
                    reuse(act, u0_ready[l], 2 * c)
                    act.activation(xc[l][:, h * HALF:(h + 1) * HALF], RING[l][h][:, 0:HALF], ACT.Silu,
                                   bias=bias_x[:, l:l + 1], scale=tapw[:, l:l + 1]).then_inc(xc_ready[l], 1)

            def silu_gate(l, c):
                for h in range(2):
                    act.wait_ge(in_done[l], 4 * c + h + 3)
                    act.activation(sg[l][:, h * HALF:(h + 1) * HALF], RING[l][h][:, 0:HALF], ACT.Silu,
                                   bias=bias_g[:, l:l + 1]).then_inc(sg_ready[l], 1)

            def states(l, c):
                for h in range(2):
                    act.wait_ge(bc_done[l], 2 * c + h + 1)
                    reuse(act, bcp_ready[l], 2 * c)
                    act.copy(bm[l][:, h * G:(h + 1) * G, :],
                             RING[l][h][0:U, :].rearrange("u (n s) -> u n s", n=G)[:, :, 0:DS])\
                        .then_inc(bm_ready[l], 1)

            def softplus_exp(l, c):
                for h in range(2):
                    act.wait_ge(dt_done[l], 2 * c + h + 1)
                    reuse(act, dt_ready[l], 2 * c)
                    act.activation(ex[l][:, h * HALF:(h + 1) * HALF], RING[l][h][:, 0:HALF], ACT.Exp,
                                   bias=dpb[:, l:l + 1]).then_inc(ex_ready[l], 1)

            def softplus_ln(l, c):
                for h in range(2):
                    act.wait_ge(exc_ready[l], 2 * c + h + 1)
                    act.activation(ex[l][:, h * HALF:(h + 1) * HALF], ex[l][:, h * HALF:(h + 1) * HALF],
                                   ACT.Ln, bias=1.0).then_inc(lg_ready[l], 1)

            def gate_exp(c):
                act.wait_ge(lsh_ready, c + 1)
                reuse(act, cw_ready, c)
                act.activation(lex[:, :, :], lsh[:, :, :], ACT.Exp).then_inc(lex_ready, 1)

            def gelu(e, c):
                for h in range(2):
                    act.wait_ge(hid_done, 2 * E * c + 2 * e + h + 1)
                    if e >= 2:
                        act.wait_ge(y_done, E * c + e - 1)
                    else:
                        reuse(act, y_done, E * c)
                    act.activation(gl[e % 2][:, h * HALF:(h + 1) * HALF], HID[h][:, 0:HALF], ACT.Gelu,
                                   bias=b1c[:, e:e + 1]).then_inc(gelu_done, 1)

            def step(h, a, b, f):
                on(a, silu_x, 0)
                on(f, at_second, 2)
                on(b, silu_x, 1)
                on(h, head_hi)
                on(a, silu_gate, 0)
                on(b, silu_gate, 1)
                act.preload_act_table_set("natural_log_exp_and_others")
                on(f, gate_exp)
                on(a, states, 0)
                on(b, states, 1)
                on(a, softplus_exp, 0)
                on(b, softplus_exp, 1)
                on(a, softplus_ln, 0)
                on(b, softplus_ln, 1)
                on(h, head_conv)
                on(h, head_tok)
                on(f, gelu, 0)
                on(h, ln_square, 0)
                on(f, gelu, 1)
                on(a, ln_square, 1)
                on(f, gelu, 2)
                on(f, gelu, 3)
                on(b, ln_square, 2)
                on(f, gelu, 4)
                on(f, gelu, 5)
                on(h, at_second, 0)
                on(f, gelu, 6)
                on(a, at_second, 1)
                on(f, gelu, 7)

            act.wait_ge(weights_ready, 1)
            run_steps(act, step)

        @block.vector
        def _(dve):
            steps = [0]

            def link(ins):
                steps[0] += 1
                ins.then_inc(v_w, 1)
                dve.wait_ge(v_w, steps[0])

            dve.wait_ge(s_w, NW)
            dve.wait_ge(vcol_done, 1)
            dve.tensor_copy(vcol[:, :], bank[6][:, 0:NV]).then_inc(vcol_ready, 1)
            dve.wait_ge(vcol_ready, 1)
            link(dve.tensor_scalar(ph[:, 0, :], ph[:, 0, :], PI / 2, None, ALU.add))
            link(dve.tensor_scalar(cs[:, :, :], ph[:, :, :], 0.5 / PI, ROUND, ALU.mult, ALU.add))
            link(dve.tensor_scalar(cs[:, :, :], cs[:, :, :], -ROUND, None, ALU.add))
            link(dve.scalar_tensor_tensor(phk[:, :, :], cs[:, :, :], -TWO_PI_HI, ph[:, :, :], ALU.mult, ALU.add))
            link(dve.scalar_tensor_tensor(phk[:, :, :], cs[:, :, :], -TWO_PI_LO, phk[:, :, :], ALU.mult, ALU.add))
            dve.tensor_scalar(phk[:, :, :], phk[:, :, :], 3.1415925, -3.1415925, ALU.min, ALU.max)\
                .then_inc(angles_ready, 1)
            link(dve.memset(wk[:, :, :], 0.0))
            dve.memset(xh[:, :, UI:UI + 1].bitcast(F32), 0.0)
            dve.memset(xl[:, :, UI:UI + 1].bitcast(F32), 0.0)
            for l in range(NL):
                link(dve.tensor_scalar(inf[:, l, :], inw[:, l, :], lnw[:, l:l + 1], None, ALU.mult))
            link(dve.tensor_copy(inh[:, :, :], inf[:, :, :]))
            dve.tensor_tensor(inl[:, :, :], inf[:, :, :], inh[:, :, :].bitcast(F32), ALU.subtract)
            link(dve.tensor_copy(w1h[:, :, :], w1f[:, :, :]))
            dve.tensor_tensor(w1l[:, :, :], w1f[:, :, :], w1h[:, :, :].bitcast(F32), ALU.subtract)
            link(dve.tensor_copy(gw2[:, 0, :], gwf[:, :]))
            dve.tensor_tensor(gw2[:, 1, :], gwf[:, :], gw2[:, 0, :].bitcast(F32), ALU.subtract)
            dve.wait_ge(sin_ready, 1)

            def angle(n):
                return cs[:, n, :].rearrange("o (k a) -> o k a", a=1).broadcast_to([COUT, K, CIN])

            link(dve.tensor_tensor(wk[:, 1:K + 1, :], wr_s[:, :].rearrange("o (i k) -> o k i", k=K), angle(0), ALU.mult))
            link(dve.tensor_tensor(wk2[:, :, :], wi_s[:, :].rearrange("o (i k) -> o k i", k=K), angle(1), ALU.mult))
            dve.tensor_tensor(wk[:, 1:K + 1, :], wk[:, 1:K + 1, :], wk2[:, :, :], ALU.subtract).then_inc(wk_ready, 1)
            dve.wait_ge(xpT_done, 1)
            dve.tensor_copy(xpT[:, :, :], bank[4][0:RK, 0:NL * DI].rearrange("r (l d) -> r l d", l=NL))\
                .then_inc(xpT_ready, 1)
            dve.wait_ge(inbias_done, 1)
            link(dve.tensor_tensor(inb[:, :, :], inb[:, :, :],
                                   bank[3][:, 0:2 * NL].rearrange("d (l h) -> d l h", l=NL), ALU.add))
            link(dve.tensor_copy(bias_g[:, :], inb[:, :, 1]))
            link(dve.tensor_tensor(bias_s[:, :], inb[:, :, 0], tapw[:, :], ALU.mult))
            link(dve.tensor_tensor(bias_x[:, :], bias_s[:, :], tapb[:, :], ALU.add))
            dve.wait_ge(wdt_done, 1)
            link(dve.tensor_copy(wdt[:, :, :], bank[5][:, 0:NL * DI].rearrange("r (l d) -> r l d", l=NL)))
            dve.wait_ge(cwp_done, 1)
            for b in range(3):
                j0, j1 = 4 * b, min(4 * b + 4, JT)
                link(dve.tensor_copy(cwh[:, j0:j1, :],
                                     bank[b][:, 0:(j1 - j0) * 128].rearrange("p (j m) -> p j m", m=128)))
                link(dve.tensor_tensor(cwl[:, j0:j1, :],
                                       bank[b][:, 0:(j1 - j0) * 128].rearrange("p (j m) -> p j m", m=128),
                                       cwh[:, j0:j1, :].bitcast(F32), ALU.subtract))
            dve.nop().then_inc(weights_ready, 1)

            def td(a):
                return a.rearrange("u (n d) -> u n d", d=D)

            def bcast(a, w=D):
                return a.rearrange("u (n a) -> u n a", a=1).broadcast_to([U, NB, w])

            def head_lo(c):
                dve.wait_ge(xh_ready, c + 1)
                reuse(dve, conv_done, c)
                dve.tensor_tensor(xl[:, :, 0:UI], HEAD[:, 0:G * UI].rearrange("p (g v) -> p g v", g=G),
                                  xh[:, :, 0:UI].bitcast(F32), ALU.subtract).then_inc(xl_ready, 1)

            def ln_center(i, c):
                src = z[i - 1] if i else ct
                if i == 0:
                    dve.wait_ge(c_saved, c + 1)
                    reuse(dve, base_part[0], c)
                else:
                    dve.wait_ge(z_ready[i - 1], c + 1)
                reuse(dve, ln_d[i], c)
                dve.reduce_sum(lnsum[:, i, :], td(src[:, :]), AX.X).then_inc(ln_sum[i], 1)
                dve.wait_ge(ln_sum[i], c + 1)
                reuse(dve, ln_sq[i], c)
                reuse(dve, ln_a[i], c)
                reuse(dve, ln_hi[i], c)
                dve.scalar_tensor_tensor(td(lnd[:, i, :]), bcast(lnsum[:, i, :]), -1.0 / D, td(src[:, :]),
                                         ALU.mult, ALU.add).then_inc(ln_d[i], 1)

            def ln_variance(i, c):
                dve.wait_ge(ln_sq[i], c + 1)
                reuse(dve, ln_r[i], c)
                dve.reduce_sum(lnvar[:, i, :], td(lnsq[:, i, :]), AX.X).then_inc(ln_var[i], 1)
                dve.wait_ge(ln_var[i], c + 1)
                if i:
                    dve.tensor_scalar(lnve[:, i, :], lnvar[:, i, :], 1.0 / D, EPS, ALU.mult, ALU.add)\
                        .then_inc(ln_ve[i], 1)
                    return
                dve.tensor_scalar(lnve[:, OUTER, :], lnvar[:, i, :], 1.0 / D, EPS, ALU.mult, ALU.add)
                dve.tensor_scalar(lnve[:, i, :], lnvar[:, i, :], (1.0 + EPS) / D, EPS * EPS, ALU.mult, ALU.add)\
                    .then_inc(ln_ve[i], 1)

            def ln_scale(i, c):
                dve.wait_ge(ln_r[i], c + 1)
                reuse(dve, ln_lo[i], c)
                dve.tensor_tensor(td(lna[:, i, :]), td(lnd[:, i, :]), bcast(lnr[:, i, :]),
                                  ALU.mult).then_inc(ln_a[i], 1)

            def ln_split(i, c):
                dve.wait_ge(ln_hi[i], c + 1)
                dve.wait_ge(ln_a[i], c + 1)
                reuse(dve, t2_done[i], 2 * c)
                dve.tensor_tensor(lhl[:, i, :, D:2 * D], td(lna[:, i, :]), lhl[:, i, :, 0:D],
                                  ALU.subtract).then_inc(ln_lo[i], 1)

            def at_first(i, c):
                dve.wait_ge(t2_done[i], 2 * c + 1)
                if i < 2:
                    reuse(dve, in_done[i], 4 * c)
                else:
                    reuse(dve, hid_done, 2 * E * c)
                    reuse(dve, gate_done, c)
                dve.tensor_copy(at[i][:, 0:HALF], src_of(i)[0][:, 0:HALF]).then_inc(at_a[i], 1)

            def states(l, c):
                for h in range(2):
                    dve.wait_ge(bm_ready[l], 2 * c + h + 1)
                    reuse(dve, bc_ready[l], c)
                    dve.tensor_tensor(bcp[l][:, h * G:(h + 1) * G, :],
                                      RING[l][h][0:U, :].rearrange("u (n s) -> u n s", n=G)[:, :, DS:2 * DS],
                                      bm[l][:, h * G:(h + 1) * G, :], ALU.mult).then_inc(bcp_ready[l], 1)
                dve.wait_ge(bcp_ready[l], 2 * c + 2)
                reuse(dve, spread_done[l], 2 * c)
                dve.reduce_sum(bc[l][:, :], bcp[l][:, :, :], AX.X).then_inc(bc_ready[l], 1)

            def clamp(l, c):
                for h in range(2):
                    cols = slice(h * HALF, (h + 1) * HALF)
                    dve.wait_ge(ex_ready[l], 2 * c + h + 1)
                    dve.tensor_scalar(ex[l][:, cols], ex[l][:, cols], SOFTPLUS_CAP, None, ALU.min)\
                        .then_inc(exc_ready[l], 1)

            def steps_of_time(l, c):
                for h in range(2):
                    cols = slice(h * HALF, (h + 1) * HALF)
                    dve.wait_ge(lg_ready[l], 2 * c + h + 1)
                    reuse(dve, o_done[l], c)
                    dve.scalar_tensor_tensor(dt[l][:, cols], RING[l][h][:, 0:HALF], dpb[:, l:l + 1], ex[l][:, cols],
                                             ALU.add, ALU.max).then_inc(dt_ready[l], 1)

            def through_state(l, c):
                for h in range(2):
                    cols = slice(h * HALF, (h + 1) * HALF)
                    dve.wait_ge(spread_done[l], 2 * c + h + 1)
                    dve.wait_ge(dt_ready[l], 2 * c + h + 1)
                    dve.tensor_tensor(dt[l][:, cols], RING[l][h][:, 0:HALF], dt[l][:, cols], ALU.mult)\
                        .then_inc(dbc_ready[l], 1)
                for h in range(2):
                    cols = slice(h * HALF, (h + 1) * HALF)
                    dve.wait_ge(dbc_ready[l], 2 * c + h + 1)
                    dve.wait_ge(u0_ready[l], 2 * c + h + 1)
                    dve.scalar_tensor_tensor(dt[l][:, cols], dt[l][:, cols], dpar[:, l:l + 1], u0[l][:, cols],
                                             ALU.add, ALU.mult).then_inc(u1_ready[l], 1)

            def layer_out(l, c):
                dve.wait_ge(o_done[l], c + 1)
                dve.wait_ge(base_ready[l], c + 1)
                reuse(dve, ln_d[l + 1], c)
                if l == 0:
                    reuse(dve, base_ready[1], c)
                else:
                    reuse(dve, acc_init, c)
                dve.tensor_tensor(z[l][:, :], RING[l][0][0:U, :], base[:, l, :], ALU.add).then_inc(z_ready[l], 1)

            NGS = 14
            at_step = [0]

            def gate_link(c, ins):
                at_step[0] += 1
                ins.then_inc(gate_step, 1)
                dve.wait_ge(gate_step, c * NGS + at_step[0])

            def spread(a):
                return bcast(a[:, :], E)

            def gate_pick(c):
                ranks = rank[:, :].rearrange("u (a e) -> u a e", a=1).broadcast_to([U, NB, E])
                at_step[0] = 0
                dve.wait_ge(gate_done, c + 1)
                logits = YB[0:U, 0:2 * NB * E].rearrange("u (n k e) -> u k n e", k=2, e=E)
                gate_link(c, dve.tensor_tensor(lgh[:, :, :], logits[:, 0],
                                               gbr[:, :].rearrange("u (a e) -> u a e", a=1).broadcast_to([U, NB, E]),
                                               ALU.add))
                gate_link(c, dve.tensor_tensor(lgt[:, :, :], logits[:, 1], lgh[:, :, :], ALU.add))
                gate_link(c, dve.reduce_max(lmx[:, :], lgt[:, :, :], AX.X))
                reuse(dve, lex_ready, c)
                dve.tensor_tensor(lsh[:, :, :], lgt[:, :, :], spread(lmx), ALU.subtract).then_inc(lsh_ready, 1)
                dve.wait_ge(lsh_ready, c + 1)
                gate_link(c, dve.scalar_tensor_tensor(lcd[:, :, :], lsh[:, :, :], 0.0, ranks, ALU.is_equal, ALU.mult))
                gate_link(c, dve.reduce_max(lkx[:, :], lcd[:, :, :], AX.X))
                gate_link(c, dve.tensor_tensor(lhot[:, :, :], lcd[:, :, :], spread(lkx), ALU.is_equal))
                gate_link(c, dve.scalar_tensor_tensor(lg2[:, :, :], lhot[:, :, :], LOGIT_DROP, lsh[:, :, :],
                                                      ALU.mult, ALU.add))
                gate_link(c, dve.reduce_max(lmx2[:, :], lg2[:, :, :], AX.X))
                gate_link(c, dve.tensor_tensor(leq2[:, :, :], lg2[:, :, :], spread(lmx2), ALU.is_equal))
                gate_link(c, dve.tensor_tensor(lcd2[:, :, :], leq2[:, :, :], ranks, ALU.mult))
                gate_link(c, dve.reduce_max(lkx2[:, :], lcd2[:, :, :], AX.X))
                gate_link(c, dve.tensor_tensor(lhot2[:, :, :], lcd2[:, :, :], spread(lkx2), ALU.is_equal))
                dve.tensor_tensor(lsel[:, :, :], lhot[:, :, :], lhot2[:, :, :], ALU.add)

            def gate_weigh(c):
                dve.wait_ge(lex_ready, c + 1)
                gate_link(c, dve.reduce_sum(lsm[:, :], lex[:, :, :], AX.X))
                gate_link(c, dve.reciprocal(lrc[:, :], lsm[:, :]))
                dve.tensor_tensor(lpw[:, :, :], lex[:, :, :], spread(lrc), ALU.mult).then_inc(gate_end, 1)
                dve.wait_ge(gate_end, c + 1)
                assert at_step[0] == NGS
                reuse(dve, py_ready, E * c)
                dve.tensor_tensor(cwt[:, :, 0:E], lpw[:, :, :], lsel[:, :, :], ALU.mult).then_inc(cw_ready, 1)

            def expert_base(c):
                dve.wait_ge(cwT_done, c + 1)
                reuse(dve, b2_done, c)
                dve.tensor_copy(cwT[:, :], YB[:, 0:U]).then_inc(cwT_ready, 1)

            def acc_start(c):
                dve.wait_ge(b2_done, c + 1)
                reuse(dve, s_out, 32 * c)
                dve.tensor_tensor(acc[:, :], YB[0:U, :], z[1][:, :], ALU.add).then_inc(acc_init, 1)

            def product(e, c):
                dve.wait_ge(y_done, c * E + e + 1)
                if e >= NPY:
                    dve.wait_ge(acc_add, c * E + e - NPY + 1)
                else:
                    reuse(dve, acc_add, c * E)
                dve.tensor_tensor(td(py[e % NPY][:, :]), td(YBANK[e % 2][0:U, :]),
                                  cwt[:, :, e:e + 1].broadcast_to([U, NB, D]), ALU.mult).then_inc(py_ready, 1)

            def step(h, a, b, f):
                on(f, at_first, 2)
                on(h, head_lo)
                on(f, gate_pick)
                on(a, states, 0)
                on(b, states, 1)
                on(f, gate_weigh)
                on(a, clamp, 0)
                on(b, clamp, 1)
                on(f, expert_base)
                on(a, steps_of_time, 0)
                on(b, steps_of_time, 1)
                on(a, through_state, 0)
                on(b, through_state, 1)
                on(f, acc_start)
                on(h, ln_center, 0)
                on(a, layer_out, 0)
                on(a, ln_center, 1)
                on(h, ln_variance, 0)
                on(f, product, 0)
                on(b, layer_out, 1)
                on(a, ln_variance, 1)
                on(h, ln_scale, 0)
                on(h, ln_split, 0)
                on(f, product, 1)
                on(b, ln_center, 2)
                on(a, ln_scale, 1)
                on(a, ln_split, 1)
                on(f, product, 2)
                on(b, ln_variance, 2)
                on(f, product, 3)
                on(b, ln_scale, 2)
                on(b, ln_split, 2)
                on(f, product, 4)
                on(h, at_first, 0)
                on(f, product, 5)
                on(a, at_first, 1)
                on(f, product, 6)
                on(f, product, 7)

            run_steps(dve, step)

        @block.tensor
        def _(pe):
            pe.wait_ge(s_id, 2)
            pe.wait_ge(s_w, NW)
            pe.transpose(bank[6][:, 0:NV], vrow[:, :], ident[0:NV, 0:NV]).then_inc(vcol_done, 1)
            pe.wait_ge(vcol_ready, 1)
            for l in range(NL):
                for h in range(2):
                    mm = pe.matmul(bank[3][:, 2 * l + h:2 * l + h + 1], inw[0:D, l, h * DI:(h + 1) * DI],
                                   lnb[0:D, l:l + 1], start=True, stop=True)
            mm.then_inc(inbias_done, 1)
            for l in range(NL):
                mm = pe.transpose(bank[4][0:RK, l * DI:(l + 1) * DI], xpw[:, l, 0:RK], ident[:, :])
            mm.then_inc(xpT_done, 1)
            pe.wait_ge(xpT_ready, 1)
            for l in range(NL):
                mm = pe.matmul(bank[5][:, l * DI:(l + 1) * DI], xpT[:, l, :], dpw[:, l, :], start=True, stop=True)
            mm.then_inc(wdt_done, 1)
            pe.wait_ge(wk_ready, 1)
            for j in range(JT):
                for p in range(2):
                    mm = pe.transpose(bank[j // 4][:, (j % 4) * 128 + p * COUT:(j % 4) * 128 + (p + 1) * COUT],
                                      wk[:, 2 * j + 1 - p:2 * j + 3 - p, :].rearrange("o k i -> o (k i)"),
                                      ident[0:COUT, 0:COUT])
            mm.then_inc(cwp_done, 1)
            pe.wait_ge(weights_ready, 1)

            def cols(n):
                return slice(n * U, (n + 1) * U)

            def transpose_x(c):
                pe.wait_ge(s_x, 16 * (c + 1))
                reuse(pe, c_saved, c)
                if not isinstance(c, int) or c > 3:
                    pe.wait_ge(py_ready, E * (c - 3))
                for g in range(G):
                    mm = pe.transpose(HEAD[:, g * UI:(g + 1) * UI], xs[:, g, :], ident[0:UI, 0:UI])
                mm.then_inc(xt_ready, 1)

            def conv(part, c):
                w, v = ((cwh, xh), (cwl, xh), (cwh, xl))[part]
                if part == 0:
                    pe.wait_ge(xl_ready, c + 1)
                for j in range(JT):
                    mm = pe.matmul(HEAD[:, 0:G * U], w[:, j, :], v[:, :, j:j + U],
                                   start=(part == 0 and j == 0), stop=(part == 2 and j == JT - 1))
                if part == 2:
                    mm.then_inc(conv_done, 1)

            def transpose_c(c):
                pe.wait_ge(cf_ready, c + 1)
                for g in range(G):
                    mm = pe.transpose(HEAD[0:U, g * 128:(g + 1) * 128], cf[:, g, :], ident[:, :])
                mm.then_inc(t1_done, 1)

            def transpose_rows(i, c):
                to = src_of(i)
                pe.wait_ge(ln_lo[i], c + 1)
                for h in range(2):
                    if i < 2:
                        reuse(pe, [z_ready[i], dbc_ready[i]][h], c * (1 + h))
                    else:
                        reuse(pe, gelu_done, 2 * E * c)
                    for n in range(G):
                        mm = pe.transpose(to[h][:, cols(n)], lhl[:, i, h * G + n, :], ident[0:U, 0:U])
                    mm.then_inc(t2_done[i], 1)

            def project_in(l, m, c):
                for h in range(2):
                    if m:
                        pe.wait_ge(xc_ready[l], 2 * c + h + 1)
                    else:
                        pe.wait_ge([at_a, at_b][h][l], c + 1)
                    for n, w in enumerate((inh, inl)):
                        mm = pe.matmul(RING[l][h][:, 0:HALF], w[:, l, m * DI:(m + 1) * DI],
                                       at[l][:, h * HALF:(h + 1) * HALF], start=(n == 0), stop=(n == 1))
                    mm.then_inc(in_done[l], 1)

            def project_states(l, c):
                pe.wait_ge(xc_ready[l], 2 * c + 2)
                for h in range(2):
                    pe.wait_ge(sg_ready[l], 2 * c + h + 1)
                    for n in range(G):
                        mm = pe.matmul(RING[l][h][0:U, n * 128:(n + 1) * 128], xc[l][:, cols(h * G + n)],
                                       xpw[:, l, RK:RK + 2 * DS], start=True, stop=True)
                    mm.then_inc(bc_done[l], 1)

            def project_dt(l, c):
                for h in range(2):
                    pe.wait_ge(bcp_ready[l], 2 * c + h + 1)
                    pe.matmul(RING[l][h][:, 0:HALF], wdt[:, l, :], xc[l][:, h * HALF:(h + 1) * HALF],
                              start=True, stop=True).then_inc(dt_done[l], 1)

            def spread_states(l, c):
                for h in range(2):
                    pe.wait_ge(dt_ready[l], 2 * c + h + 1)
                    pe.wait_ge(bc_ready[l], c + 1)
                    for n in range(h * G, (h + 1) * G):
                        mm = pe.transpose(RING[l][h][:, cols(n - h * G)], bc[l][:, n:n + 1].broadcast_to([U, DI]),
                                          ident[0:U, 0:U])
                    mm.then_inc(spread_done[l], 1)

            def project_out(l, c):
                pe.wait_ge(dbc_ready[l], 2 * c + 1)
                pe.wait_ge(u1_ready[l], 2 * c + 2)
                for n in range(NB):
                    mm = pe.matmul(RING[l][0][0:U, n * D:(n + 1) * D], dt[l][:, cols(n)], ow[:, l, :],
                                   start=True, stop=True)
                mm.then_inc(o_done[l], 1)

            def gate(c):
                pe.wait_ge(at_a[2], c + 1)
                pe.wait_ge(at_b[2], c + 1)
                reuse(pe, py_ready, E * c)
                for n in range(NB):
                    mm = pe.matmul(YB[0:U, n * 2 * E:(n + 1) * 2 * E], at[2][:, cols(n)],
                                   gw2[:, :, :].rearrange("d k e -> d (k e)"), start=True, stop=True)
                mm.then_inc(gate_done, 1)

            def expert_weights(c):
                pe.wait_ge(cw_ready, c + 1)
                pe.transpose(YB[:, 0:U], cwt[:, :, :].rearrange("u n e -> u (n e)"), ident[0:U, 0:U])\
                    .then_inc(cwT_done, 1)

            def expert_bias(c):
                pe.wait_ge(cwT_ready, c + 1)
                pe.matmul(YB[0:U, :], cwT[:, :], b2d[:, :, :].rearrange("k n d -> k (n d)"),
                          start=True, stop=True).then_inc(b2_done, 1)

            def hidden(e, c):
                for h in range(2):
                    if e:
                        pe.wait_ge(gelu_done, 2 * E * c + 2 * e + h - 1)
                    for k, w in enumerate((w1h, w1l)):
                        mm = pe.matmul(HID[h][:, 0:HALF], w[:, e, :], at[2][:, h * HALF:(h + 1) * HALF],
                                       start=(k == 0), stop=(k == 1))
                    mm.then_inc(hid_done, 1)

            def expert_out(e, c, head):
                if e >= 2:
                    pe.wait_ge(py_ready, E * c + e - 1)
                elif e == 0:
                    pe.wait_ge(acc_init, c + 1)
                elif head is not None:
                    pe.wait_ge(c_saved, head + 1)
                else:
                    reuse(pe, py_ready, E * c)
                pe.wait_ge(gelu_done, 2 * E * c + 2 * e + 2)
                for n in range(NB):
                    mm = pe.matmul(YBANK[e % 2][0:U, n * D:(n + 1) * D], gl[e % 2][:, cols(n)], w2s[:, e, :],
                                   start=True, stop=True)
                mm.then_inc(y_done, 1)

            def experts(e0, e1, c, head):
                for e in range(e0, e1):
                    if e + 1 < E:
                        hidden(e + 1, c)
                    expert_out(e, c, head)

            def step(h, a, b, f):
                on(f, transpose_rows, 2)
                on(h, transpose_x)
                on(a, project_in, 0, 1)
                on(f, gate)
                on(b, project_in, 1, 1)
                on(h, conv, 0)
                on(a, project_states, 0)
                on(b, project_states, 1)
                on(a, project_dt, 0)
                on(b, project_dt, 1)
                on(f, expert_weights)
                on(h, conv, 1)
                on(h, conv, 2)
                on(a, spread_states, 0)
                on(f, expert_bias)
                on(b, spread_states, 1)
                on(f, hidden, 0)
                on(h, transpose_c)
                on(a, project_out, 0)
                on(b, project_out, 1)
                if f is not None:
                    experts(0, 5, f, h)
                on(h, transpose_rows, 0)
                if f is not None:
                    experts(5, 6, f, h)
                on(h, project_in, 0, 0)
                on(a, transpose_rows, 1)
                if f is not None:
                    experts(6, 7, f, h)
                on(a, project_in, 1, 0)
                if f is not None:
                    experts(7, 8, f, h)

            run_steps(pe, step)


_INS = ['x', 'L0_tok_w_real', 'L0_tok_w_imag', 'L0_tok_phases', 'L0_attn_ln_w', 'L0_attn_ln_b', 'L0_attn_in_w',
        'L0_attn_in_b', 'L0_attn_conv_w', 'L0_attn_conv_b', 'L0_attn_xproj_w', 'L0_attn_dtproj_w',
        'L0_attn_dtproj_b', 'L0_attn_D_param', 'L0_attn_out_w', 'L0_attn_out_b', 'L0_ffn_gate_w',
        'L0_ffn_gate_b', 'L0_ffn_W1', 'L0_ffn_b1', 'L0_ffn_W2', 'L0_ffn_b2']
_OUTS = [((64, 235, 64), 'float32')]


def kernel(**inputs):
    import numpy as _np
    import concourse.bacc as _bacc
    from concourse import mybir as _mybir
    from concourse.bass_utils import run_bass_kernel_spmd as _run

    nc = _bacc.Bacc("TRN2", target_bir_lowering=False, num_devices=1)
    arrays, args = {}, []
    for name in _INS:
        a = _np.ascontiguousarray(inputs[name])
        arrays[f"in_{name}_dram"] = a
        args.append(nc.dram_tensor(f"in_{name}_dram", a.shape, _mybir.dt.from_np(a.dtype), kind="ExternalInput").ap())
    for i, (shape, dtype) in enumerate(_OUTS):
        dt = _mybir.dt.from_np(_np.dtype(dtype))
        args.append(nc.dram_tensor(f"out_{i}_dram", shape, dt, kind="ExternalOutput").ap())
    audio_tower(nc, *args)
    r = _run(nc, [arrays], core_ids=[0])
    got = tuple(r.results[0][f"out_{i}_dram"] for i in range(len(_OUTS)))
    return got[0]
```

```python
from contextlib import ExitStack

import concourse.bass as bass
from concourse import mybir

ALU = mybir.AluOpType
ACT = mybir.ActivationFunctionType
AX = mybir.AxisListType
F32 = mybir.dt.float32
F32R = mybir.dt.float32r

EPS = 1e-5
PI = 3.14159265358979
ROUND = 12582912.0
TWO_PI_HI = 6.28125
TWO_PI_LO = 1.9353071795864769e-3
SOFTPLUS_CAP = 1e18
LOGIT_DROP = -3.0e38


def audio_tower(nc, x, w_real, w_imag, phases, ln_w, ln_b, in_w, in_b, conv_w, conv_b, xproj_w,
                dtproj_w, dtproj_b, D_param, out_w, out_b, gate_w, gate_b, W1, b1, W2, b2, out):
    B, S, CIN = x.shape
    COUT, _, K = w_real.shape
    SO = S - K + 1
    NL, D, DI2 = in_w.shape
    DI = DI2 // 2
    DS = (xproj_w.shape[2] - dtproj_w.shape[1]) // 2
    RK = dtproj_w.shape[1]
    E, _, H = W1.shape
    G = 4
    NCH = B // G
    UI = S // 2
    U = (SO + 1) // 2
    JT = K // 2 + 1
    NB = 2 * G
    HALF = NB // 2 * U
    TD = NB * D
    EP = 2 * E
    assert NB * EP == 128

    xv = x.rearrange("b (v c) i -> v b (c i)", c=2)
    out_pairs = out[:, 0:2 * (U - 1), :].rearrange("b (u c) d -> u b (c d)", c=2)
    out_last = out[:, 2 * (U - 1):SO, :].rearrange("b c d -> c b d")

    with ExitStack() as ctx:
        def sb(name, shape, dt=F32):
            return ctx.enter_context(nc.sbuf_tensor(name, shape, dt))

        def sem(name):
            return ctx.enter_context(nc.semaphore(name))

        bank = [ctx.enter_context(nc.psum_tensor(f"bank{i}", [128, 512], F32)) for i in range(8)]
        HEAD = bank[0]
        RING = [[bank[1], bank[2]], [bank[3], bank[4]]]
        HID = [bank[5], bank[6]]
        YB = bank[7]
        YBANK = [YB, HEAD]

        ident = sb("ident", [128, 128])
        NV = 8 * NL + E
        vrow = sb("vrow", [NV, 128])
        vcol = sb("vcol", [128, NV])
        inb = vcol[:, 0:2 * NL].rearrange("d (l h) -> d l h", l=NL)
        tapw, tapb, dpb, dpar = (vcol[:, (2 + i) * NL:(3 + i) * NL] for i in range(4))
        b1c = vcol[:, 6 * NL:6 * NL + E]
        lnw, lnb = (vcol[:, 6 * NL + E + i * NL:6 * NL + E + (i + 1) * NL] for i in range(2))
        wr_s = sb("wr_s", [COUT, CIN * K])
        wi_s = sb("wi_s", [COUT, CIN * K])
        ph = sb("ph", [COUT, 2, K])
        phk = sb("phk", [COUT, 2, K])
        cs = sb("cs", [COUT, 2, K])
        wk = sb("wk", [COUT, K + 3, CIN])
        wk2 = sb("wk2", [COUT, K, CIN])
        cwh = sb("cwh", [128, JT, 128], F32R)
        cwl = sb("cwl", [128, JT, 128], F32R)
        inw = sb("inw", [128, NL, DI2])
        inf = sb("inf", [128, NL, DI2])
        inh = sb("inh", [128, NL, DI2], F32R)
        inl = sb("inl", [128, NL, DI2], F32R)
        bias_g = sb("bias_g", [DI, NL])
        bias_s = sb("bias_s", [DI, NL])
        bias_x = sb("bias_x", [DI, NL])
        xpw = sb("xpw", [DI, NL, RK + 2 * DS])
        xpT = sb("xpT", [RK, NL, DI])
        dpw = sb("dpw", [RK, NL, DI])
        wdth = sb("wdth", [DI, NL, DI], F32R)
        wdtl = sb("wdtl", [DI, NL, DI], F32R)
        ow = sb("ow", [DI, NL, D])
        obr = sb("obr", [U, NL, D])
        gwf = sb("gwf", [128, E])
        gw2 = sb("gw2", [128, 2, E], F32R)
        gbr = sb("gbr", [U, E])
        rank = sb("rank", [U, E])
        w1f = sb("w1f", [128, E, H])
        w1h = sb("w1h", [128, E, H], F32R)
        w1l = sb("w1l", [128, E, H], F32R)
        w2s = sb("w2s", [H, E, D])
        b2d = sb("b2d", [128, NB, D])
        b2h = sb("b2h", [128, NB, D], F32R)
        b2l = sb("b2l", [128, NB, D], F32R)
        nhalf = sb("nhalf", [U, NB])

        NPY = 4
        OUTER = 3
        xs = sb("xs", [UI, G, 128])
        xh = sb("xh", [128, G, UI + 1], F32R)
        xl = sb("xl", [128, G, UI + 1], F32R)
        cf = sb("cf", [128, G, U])
        ct = sb("ct", [U, TD])
        lnsum = sb("lnsum", [U, 3, NB])
        lnd = sb("lnd", [U, 3, TD])
        lnsq = sb("lnsq", [U, 3, TD])
        lnvar = sb("lnvar", [U, 3, NB])
        lnve = sb("lnve", [U, 4, NB])
        lnr = sb("lnr", [U, 4, NB])
        lna = sb("lna", [U, 3, TD])
        lhl = sb("lhl", [U, 3, NB, 2 * D])
        base = sb("base", [U, 2, TD])
        base_t = sb("base_t", [U, 2, TD])
        at = [sb(f"at{i}", [128, 2 * HALF], F32R) for i in range(3)]
        xc = [sb(f"xc{i}", [DI, 2 * HALF]) for i in range(2)]
        xch = [sb(f"xch{i}", [DI, 2 * HALF], F32R) for i in range(2)]
        xcl = [sb(f"xcl{i}", [DI, 2 * HALF], F32R) for i in range(2)]
        u0 = [sb(f"u0{i}", [DI, 2 * HALF]) for i in range(2)]
        ex = [sb(f"ex{i}", [DI, 2 * HALF]) for i in range(2)]
        dt = [sb(f"dt{i}", [DI, 2 * HALF]) for i in range(2)]
        bm = [sb(f"bm{i}", [U, NB, DS]) for i in range(2)]
        bcp = [sb(f"bcp{i}", [U, NB, DS]) for i in range(2)]
        bc = [sb(f"bc{i}", [U, NB]) for i in range(2)]
        z = [sb(f"z{i}", [U, TD]) for i in range(2)]
        lgh = sb("lgh", [U, NB, E])
        lgt = sb("lgt", [U, NB, E])
        lmx = sb("lmx", [U, NB])
        lcd = sb("lcd", [U, NB, E])
        lkx = sb("lkx", [U, NB])
        lhot = sb("lhot", [U, NB, E])
        lg2 = sb("lg2", [U, NB, E])
        lmx2 = sb("lmx2", [U, NB])
        leq2 = sb("leq2", [U, NB, E])
        lcd2 = sb("lcd2", [U, NB, E])
        lkx2 = sb("lkx2", [U, NB])
        lhot2 = sb("lhot2", [U, NB, E])
        lsel = sb("lsel", [U, NB, E])
        lsh = sb("lsh", [U, NB, E])
        lex = sb("lex", [U, NB, E])
        lsm = sb("lsm", [U, NB])
        lrc = sb("lrc", [U, NB])
        lpw = sb("lpw", [U, NB, E])
        wts = sb("wts", [U, NB, E])
        cwt = sb("cwt", [U, NB, EP])
        cwT = sb("cwT", [128, U], F32R)
        gl = [sb(f"gl{i}", [H, 2 * HALF]) for i in range(2)]
        py = [sb(f"py{i}", [U, TD]) for i in range(NPY)]
        wb2 = sb("wb2", [U, TD])
        acc = sb("acc", [U, TD])

        conv_in = sem("conv_in")
        layer_in = sem("layer_in")
        expert_in = sem("expert_in")
        s_id = sem("ident_ready")
        s_pz = sem("pool_consts")
        v_w = sem("dve_weight_step")
        angles_ready = sem("angles_ready")
        sin_ready = sem("sin_ready")
        vcol_done = sem("vcol_done")
        vcol_ready = sem("vcol_ready")
        wk_ready = sem("wk_ready")
        cwp_done = sem("cwp_done")
        xpT_done = sem("xpT_done")
        xpT_ready = sem("xpT_ready")
        inbias_done = sem("inbias_done")
        wdt_done = sem("wdt_done")
        wk2_ready = sem("wk2_ready")
        cwh_ready = sem("cwh_ready")
        cwl_ready = sem("cwl_ready")
        layers_ready = sem("layers_ready")
        experts_ready = sem("experts_ready")
        s_x = sem("x_in")
        s_out = sem("out_stored")
        xt_ready = sem("xt_ready")
        xh_ready = sem("xh_ready")
        xl_ready = sem("xl_ready")
        conv_done = sem("conv_done")
        cf_ready = sem("cf_ready")
        t1_done = sem("t1_done")
        c_saved = sem("c_saved")
        ln_sum = [sem(f"ln_sum{i}") for i in range(3)]
        ln_d = [sem(f"ln_d{i}") for i in range(3)]
        ln_sq = [sem(f"ln_sq{i}") for i in range(3)]
        ln_ve = [sem(f"ln_ve{i}") for i in range(3)]
        ln_var = [sem(f"ln_var{i}") for i in range(3)]
        ln_r = [sem(f"ln_r{i}") for i in range(3)]
        ln_a = [sem(f"ln_a{i}") for i in range(3)]
        ln_hi = [sem(f"ln_hi{i}") for i in range(3)]
        ln_lo = [sem(f"ln_lo{i}") for i in range(3)]
        outer_r = sem("outer_r")
        base_part = [sem(f"base_part{i}") for i in range(2)]
        base_ready = [sem(f"base_ready{i}") for i in range(2)]
        t2_done = [sem(f"t2_done{i}") for i in range(3)]
        at_a = [sem(f"at_a{i}") for i in range(3)]
        at_b = [sem(f"at_b{i}") for i in range(3)]
        in_done = [sem(f"in_done{i}") for i in range(2)]
        xc_ready = [sem(f"xc_ready{i}") for i in range(2)]
        xch_ready = [sem(f"xch_ready{i}") for i in range(2)]
        xcl_ready = [sem(f"xcl_ready{i}") for i in range(2)]
        sg_ready = [sem(f"sg_ready{i}") for i in range(2)]
        u0_ready = [sem(f"u0_ready{i}") for i in range(2)]
        bc_done = [sem(f"bc_done{i}") for i in range(2)]
        bm_ready = [sem(f"bm_ready{i}") for i in range(2)]
        bcp_ready = [sem(f"bcp_ready{i}") for i in range(2)]
        bc_ready = [sem(f"bc_ready{i}") for i in range(2)]
        dt_done = [sem(f"dt_done{i}") for i in range(2)]
        ex_ready = [sem(f"ex_ready{i}") for i in range(2)]
        exc_ready = [sem(f"exc_ready{i}") for i in range(2)]
        lg_ready = [sem(f"lg_ready{i}") for i in range(2)]
        dt_ready = [sem(f"dt_ready{i}") for i in range(2)]
        spread_done = [sem(f"spread_done{i}") for i in range(2)]
        dbc_ready = [sem(f"dbc_ready{i}") for i in range(2)]
        u1_ready = [sem(f"u1_ready{i}") for i in range(2)]
        o_done = [sem(f"o_done{i}") for i in range(2)]
        z_ready = [sem(f"z_ready{i}") for i in range(2)]
        gate_done = sem("gate_done")
        lsh_ready = sem("lsh_ready")
        lex_ready = sem("lex_ready")
        gate_step = sem("gate_step")
        gate_end = sem("gate_end")
        cw_ready = sem("cw_ready")
        cwT_done = sem("cwT_done")
        cwT_ready = sem("cwT_ready")
        b2_done = sem("b2_done")
        b2_saved = sem("b2_saved")
        acc_init = sem("acc_init")
        hid_done = sem("hid_done")
        gelu_done = sem("gelu_done")
        y_done = sem("y_done")
        py_ready = sem("py_ready")
        acc_add = sem("acc_add")

        def reuse(eng, last, n):
            if not isinstance(n, int) or n > 0:
                eng.wait_ge(last, n)

        def on(c, stage, *which):
            if c is not None:
                stage(*which, c)

        def first(c):
            return isinstance(c, int) and c == 0

        def angle(n):
            return cs[:, n, :].rearrange("o (k a) -> o k a", a=1).broadcast_to([COUT, K, CIN])

        def tap_banks():
            for b in range((JT + 3) // 4):
                j0, j1 = 4 * b, min(4 * b + 4, JT)
                yield b, slice(j0, j1), bank[1 + b][:, 0:(j1 - j0) * 128].rearrange("p (j m) -> p j m", m=128)

        def src_of(i):
            return RING[i] if i < 2 else HID

        def run_steps(eng, step, peeled=0):
            for t in range(4):
                step(t, *(t - k if t >= k else None for k in (1, 2, 3)))
            with eng.Fori(1, NCH - 3 - peeled) as i:
                step(i + 3, i + 2, i + 1, i)
            for t in range(NCH - peeled, NCH + 3):
                step(*(t - k if t - k < NCH else None for k in range(4)))

        block = ctx.enter_context(nc.Block())

        conv_loads = [
            (ph[:, :, :], phases.rearrange("(a b k) -> a b k", a=1, b=1).broadcast_to([COUT, 2, K])),
            (wr_s[:, :], w_real.rearrange("o i k -> o (i k)")),
            (wi_s[:, :], w_imag.rearrange("o i k -> o (i k)")),
        ]
        layer_loads = [
            (vrow[0:2 * NL, :], in_b.rearrange("l (h d) -> (l h) d", h=2)),
            (vrow[2 * NL:3 * NL, :], conv_w[:, conv_w.shape[1] - 1, :]),
            (vrow[3 * NL:4 * NL, :], conv_b),
            (vrow[4 * NL:5 * NL, :], dtproj_b),
            (vrow[5 * NL:6 * NL, :], D_param),
            (vrow[6 * NL:6 * NL + E, :], b1),
        ]
        expert_loads = [
            (w2s[:, :, :], W2.rearrange("e h d -> h e d")),
            (gbr[:, :], gate_b.rearrange("(a e) -> a e", a=1).broadcast_to([U, E])),
        ]
        for h in range(2):
            layer_loads.append((vrow[6 * NL + E:7 * NL + E, h * D:(h + 1) * D], ln_w))
            layer_loads.append((vrow[7 * NL + E:8 * NL + E, h * D:(h + 1) * D], ln_b))
            layer_loads.append((inw[h * D:(h + 1) * D, :, :], in_w.rearrange("l d n -> d l n")))
            expert_loads.append((gwf[h * D:(h + 1) * D, :], gate_w))
            expert_loads.append((w1f[h * D:(h + 1) * D, :, :], W1.rearrange("e d h -> d e h")))
        layer_loads += [
            (xpw[:, :, :], xproj_w.rearrange("l d n -> d l n")),
            (dpw[:, :, :], dtproj_w.rearrange("l r d -> r l d")),
            (ow[:, :, :], out_w.rearrange("l d n -> d l n")),
        ]
        for l in range(NL):
            layer_loads.append((obr[:, l, :], out_b[l:l + 1, :].broadcast_to([U, D])))
        ALL_CONV = 16 * len(conv_loads)
        ALL_LAYER = 16 * len(layer_loads)
        ALL_EXPERT = 16 * (len(expert_loads) + 2 * NB)

        @block.sync
        def _(sp):
            def load(c):
                reuse(sp, xt_ready, c)
                sp.dma_start(xs[:, :, :], xv[:, bass.ds(c * G, G), :]).then_inc(s_x, 16)

            def store(c):
                sp.wait_ge(acc_add, (c + 1) * E)
                sp.dma_start(out_pairs[:, bass.ds(c * G, G), :],
                             acc[0:U - 1, :].rearrange("u (g n) -> u g n", g=G)).then_inc(s_out, 16)
                sp.dma_start(out_last[:, bass.ds(c * G, G), :],
                             acc[U - 1:U, :].rearrange("u (g n) -> u g n", g=G)[:, :, 0:D]).then_inc(s_out, 16)

            def step(h, a, b, f):
                if h is not None and not (isinstance(h, int) and h == NCH - 1):
                    load(h + 1)
                if f is not None:
                    store(f)

            for dst, src in conv_loads:
                sp.dma_start(dst, src).then_inc(conv_in, 16)
            load(0)
            for dst, src in layer_loads:
                sp.dma_start(dst, src).then_inc(layer_in, 16)
            for dst, src in expert_loads:
                sp.dma_start(dst, src).then_inc(expert_in, 16)
            sp.wait_ge(s_pz, 1)
            for n in range(NB):
                for r in range(n * EP, (n + 1) * EP, E):
                    sp.dma_start(b2d[r:r + E, n, :], b2).then_inc(expert_in, 16)
            run_steps(sp, step, peeled=1)
            sp.wait_ge(s_out, 32 * NCH)

        @block.gpsimd
        def _(pool):
            pool.memset(b2d[:, :, :], 0.0).then_inc(s_pz, 1)
            pool.memset(nhalf[:, :], -0.5).then_inc(s_pz, 1)
            for e in range(E):
                pool.memset(rank[:, e:e + 1], float(E - e)).then_inc(s_pz, 1)
            pool.memset(ident[:, :], 0.0).then_inc(s_id, 1)
            pool.wait_ge(s_id, 1)
            pool.affine_select(out=ident[:, :], in_=ident[:, :], compare_op=ALU.not_equal, fill=1.0,
                               base=0, pattern=[[-1, 128]], channel_multiplier=1).then_inc(s_id, 1)
            pool.wait_ge(s_pz, 2 + E)
            pool.wait_ge(conv_in, ALL_CONV)
            pool.wait_ge(sin_ready, 1)
            pool.tensor_tensor(wk2[:, :, :], wi_s[:, :].rearrange("o (i k) -> o k i", k=K), angle(1), ALU.mult)\
                .then_inc(wk2_ready, 1)
            pool.wait_ge(layer_in, ALL_LAYER)

            def bcast(a):
                return a.rearrange("u (n a) -> u n a", a=1).broadcast_to([U, NB, D])

            def td(a):
                return a.rearrange("u (n d) -> u n d", d=D)

            def ln_rows(i, c):
                pool.wait_ge(ln_ve[i], c + 1)
                reuse(pool, ln_a[i], c)
                pool.tensor_tensor(lnr[:, i, :], lnve[:, i, :], nhalf[:, :], ALU.pow).then_inc(ln_r[i], 1)

            def ln_split(i, c):
                pool.wait_ge(ln_r[i], c + 1)
                reuse(pool, t2_done[i], 2 * c)
                reuse(pool, ln_lo[i], c)
                pool.tensor_tensor(lhl[:, i, :, 0:D].bitcast(F32R), td(lnd[:, i, :]),
                                   bcast(lnr[:, i, :]), ALU.mult).then_inc(ln_hi[i], 1)

            def base0(c):
                pool.wait_ge(ln_ve[0], c + 1)
                reuse(pool, base_part[0], c)
                pool.tensor_tensor(lnr[:, OUTER, :], lnve[:, OUTER, :], nhalf[:, :], ALU.pow).then_inc(outer_r, 1)
                pool.wait_ge(outer_r, c + 1)
                reuse(pool, base_ready[0], c)
                pool.tensor_tensor(td(base_t[:, 0, :]), td(lnd[:, 0, :]), bcast(lnr[:, OUTER, :]), ALU.mult)\
                    .then_inc(base_part[0], 1)
                pool.wait_ge(base_part[0], c + 1)
                reuse(pool, z_ready[0], c)
                pool.tensor_tensor(td(base[:, 0, :]), td(base_t[:, 0, :]),
                                   obr[:, 0:1, :].broadcast_to([U, NB, D]), ALU.add).then_inc(base_ready[0], 1)

            def base1_part(c):
                pool.wait_ge(c_saved, c + 1)
                reuse(pool, base_ready[1], c)
                pool.tensor_tensor(td(base_t[:, 1, :]), td(ct[:, :]), obr[:, 1:2, :].broadcast_to([U, NB, D]),
                                   ALU.add).then_inc(base_part[1], 1)

            def base1(c):
                pool.wait_ge(base_part[1], c + 1)
                pool.wait_ge(z_ready[0], c + 1)
                reuse(pool, z_ready[1], c)
                pool.tensor_tensor(base[:, 1, :], base_t[:, 1, :], z[0][:, :], ALU.add).then_inc(base_ready[1], 1)

            def conv_lo(l, c):
                for h in range(2):
                    cols = slice(h * HALF, (h + 1) * HALF)
                    pool.wait_ge(xch_ready[l], 2 * c + h + 1)
                    reuse(pool, dt_done[l], 2 * c)
                    pool.tensor_tensor(xcl[l][:, cols], xc[l][:, cols], xch[l][:, cols].bitcast(F32), ALU.subtract)\
                        .then_inc(xcl_ready[l], 1)

            def gated(l, c):
                for h in range(2):
                    cols = slice(h * HALF, (h + 1) * HALF)
                    pool.wait_ge(xc_ready[l], 2 * c + h + 1)
                    pool.wait_ge(sg_ready[l], 2 * c + h + 1)
                    pool.tensor_tensor(u0[l][:, cols], xc[l][:, cols], u0[l][:, cols], ALU.mult)\
                        .then_inc(u0_ready[l], 1)

            def acc_start(c):
                pool.wait_ge(b2_saved, c + 1)
                pool.wait_ge(z_ready[1], c + 1)
                reuse(pool, s_out, 32 * c)
                pool.tensor_tensor(acc[:, :], wb2[:, :], z[1][:, :], ALU.add).then_inc(acc_init, 1)

            def add_expert(e, c):
                pool.wait_ge(py_ready, c * E + e + 1)
                if e == 0:
                    pool.wait_ge(acc_init, c + 1)
                reuse(pool, acc_add, c * E + e)
                pool.tensor_tensor(acc[:, :], acc[:, :], py[e % NPY][:, :], ALU.add).then_inc(acc_add, 1)

            def step(h, a, b, f):
                on(a, conv_lo, 0)
                on(b, conv_lo, 1)
                on(a, gated, 0)
                on(b, gated, 1)
                on(b, base1)
                on(a, base0)
                on(a, base1_part)
                on(f, acc_start)
                on(h, ln_rows, 0)
                on(h, ln_split, 0)
                on(a, ln_rows, 1)
                on(f, add_expert, 0)
                on(a, ln_split, 1)
                on(f, add_expert, 1)
                on(b, ln_rows, 2)
                on(f, add_expert, 2)
                on(b, ln_split, 2)
                for e in range(3, E):
                    on(f, add_expert, e)

            run_steps(pool, step)

        @block.scalar
        def _(act):
            act.wait_ge(angles_ready, 1)
            act.activation(cs[:, :, :], phk[:, :, :], ACT.Sin).then_inc(sin_ready, 1)
            for b, taps, psum in tap_banks():
                act.wait_ge(cwp_done, b + 1)
                act.copy(cwh[:, taps, :], psum).then_inc(cwh_ready, 1)

            def head_hi(c):
                act.wait_ge(xt_ready, c + 1)
                reuse(act, conv_done, c)
                act.copy(xh[:, :, 0:UI], HEAD[:, 0:G * UI].rearrange("p (g v) -> p g v", g=G))\
                    .then_inc(xh_ready, 1)

            def head_conv(c):
                act.wait_ge(conv_done, c + 1)
                reuse(act, t1_done, c)
                act.copy(cf[:, :, :], HEAD[:, 0:G * U].rearrange("p (g u) -> p g u", g=G)).then_inc(cf_ready, 1)

            def head_tok(c):
                act.wait_ge(t1_done, c + 1)
                reuse(act, ln_d[0], c)
                reuse(act, base_part[1], c)
                act.copy(ct[:, :], HEAD[0:U, :]).then_inc(c_saved, 1)

            def ln_square(i, c):
                act.wait_ge(ln_d[i], c + 1)
                reuse(act, ln_var[i], c)
                act.activation(lnsq[:, i, :], lnd[:, i, :], ACT.Square).then_inc(ln_sq[i], 1)

            def at_second(i, c):
                act.wait_ge(t2_done[i], 2 * c + 2)
                if i < 2:
                    reuse(act, in_done[i], 4 * c)
                else:
                    reuse(act, hid_done, 2 * E * c)
                    reuse(act, gate_done, c)
                act.copy(at[i][:, HALF:2 * HALF], src_of(i)[1][:, 0:HALF]).then_inc(at_b[i], 1)

            def silu_x(l, c):
                for h in range(2):
                    act.wait_ge(in_done[l], 4 * c + h + 1)
                    reuse(act, bc_done[l], 2 * c)
                    reuse(act, xch_ready[l], 2 * c)
                    reuse(act, u0_ready[l], 2 * c)
                    act.activation(xc[l][:, h * HALF:(h + 1) * HALF], RING[l][h][:, 0:HALF], ACT.Silu,
                                   bias=bias_x[:, l:l + 1], scale=tapw[:, l:l + 1]).then_inc(xc_ready[l], 1)

            def silu_gate(l, c):
                for h in range(2):
                    act.wait_ge(in_done[l], 4 * c + h + 3)
                    reuse(act, u1_ready[l], 2 * c)
                    act.activation(u0[l][:, h * HALF:(h + 1) * HALF], RING[l][h][:, 0:HALF], ACT.Silu,
                                   bias=bias_g[:, l:l + 1]).then_inc(sg_ready[l], 1)

            def states(l, c):
                for h in range(2):
                    act.wait_ge(bc_done[l], 2 * c + h + 1)
                    reuse(act, bcp_ready[l], 2 * c)
                    act.copy(bm[l][:, h * G:(h + 1) * G, :],
                             RING[l][h][0:U, :].rearrange("u (n s) -> u n s", n=G)[:, :, 0:DS])\
                        .then_inc(bm_ready[l], 1)

            def softplus_exp(l, c):
                for h in range(2):
                    act.wait_ge(dt_done[l], 2 * c + h + 1)
                    reuse(act, dt_ready[l], 2 * c)
                    act.activation(ex[l][:, h * HALF:(h + 1) * HALF], RING[l][h][:, 0:HALF], ACT.Exp,
                                   bias=dpb[:, l:l + 1]).then_inc(ex_ready[l], 1)

            def softplus_ln(l, c):
                for h in range(2):
                    act.wait_ge(exc_ready[l], 2 * c + h + 1)
                    act.activation(ex[l][:, h * HALF:(h + 1) * HALF], ex[l][:, h * HALF:(h + 1) * HALF],
                                   ACT.Ln, bias=1.0).then_inc(lg_ready[l], 1)

            def gate_exp(c):
                act.wait_ge(lsh_ready, c + 1)
                reuse(act, cw_ready, c)
                act.activation(lex[:, :, :], lsh[:, :, :], ACT.Exp).then_inc(lex_ready, 1)

            def bias_out(c):
                act.wait_ge(b2_done, c + 1)
                reuse(act, acc_init, c)
                act.copy(wb2[:, :], YB[0:U, :]).then_inc(b2_saved, 1)

            def gelu(e, c):
                for h in range(2):
                    act.wait_ge(hid_done, 2 * E * c + 2 * e + h + 1)
                    if e >= 2:
                        act.wait_ge(y_done, E * c + e - 1)
                    else:
                        reuse(act, y_done, E * c)
                    act.activation(gl[e % 2][:, h * HALF:(h + 1) * HALF], HID[h][:, 0:HALF], ACT.Gelu,
                                   bias=b1c[:, e:e + 1]).then_inc(gelu_done, 1)

            def step(h, a, b, f):
                on(a, silu_x, 0)
                on(f, at_second, 2)
                on(h, head_hi)
                on(b, silu_x, 1)
                on(a, silu_gate, 0)
                on(b, silu_gate, 1)
                act.preload_act_table_set("natural_log_exp_and_others")
                on(f, gate_exp)
                on(a, states, 0)
                on(b, states, 1)
                on(a, softplus_exp, 0)
                on(b, softplus_exp, 1)
                on(a, softplus_ln, 0)
                on(b, softplus_ln, 1)
                on(h, head_conv)
                on(f, bias_out)
                on(h, head_tok)
                on(f, gelu, 0)
                on(h, ln_square, 0)
                if first(h):
                    act.wait_ge(layers_ready, 1)
                on(f, gelu, 1)
                on(a, ln_square, 1)
                on(f, gelu, 2)
                on(f, gelu, 3)
                on(b, ln_square, 2)
                on(f, gelu, 4)
                on(h, at_second, 0)
                on(f, gelu, 5)
                on(a, at_second, 1)
                on(f, gelu, 6)
                on(f, gelu, 7)

            run_steps(act, step)

        @block.vector
        def _(dve):
            steps = [0]

            def link(ins):
                steps[0] += 1
                ins.then_inc(v_w, 1)
                dve.wait_ge(v_w, steps[0])

            dve.wait_ge(conv_in, ALL_CONV)
            link(dve.tensor_scalar(ph[:, 0, :], ph[:, 0, :], PI / 2, None, ALU.add))
            link(dve.tensor_scalar(cs[:, :, :], ph[:, :, :], 0.5 / PI, ROUND, ALU.mult, ALU.add))
            link(dve.tensor_scalar(cs[:, :, :], cs[:, :, :], -ROUND, None, ALU.add))
            link(dve.scalar_tensor_tensor(phk[:, :, :], cs[:, :, :], -TWO_PI_HI, ph[:, :, :], ALU.mult, ALU.add))
            link(dve.scalar_tensor_tensor(phk[:, :, :], cs[:, :, :], -TWO_PI_LO, phk[:, :, :], ALU.mult, ALU.add))
            dve.tensor_scalar(phk[:, :, :], phk[:, :, :], 3.1415925, -3.1415925, ALU.min, ALU.max)\
                .then_inc(angles_ready, 1)
            dve.memset(wk[:, 0:1, :], 0.0)
            dve.memset(wk[:, K + 1:K + 3, :], 0.0)
            dve.memset(xh[:, :, UI:UI + 1].bitcast(F32), 0.0)
            dve.memset(xl[:, :, UI:UI + 1].bitcast(F32), 0.0)
            dve.wait_ge(sin_ready, 1)
            link(dve.tensor_tensor(wk[:, 1:K + 1, :], wr_s[:, :].rearrange("o (i k) -> o k i", k=K), angle(0), ALU.mult))
            dve.wait_ge(wk2_ready, 1)
            dve.tensor_tensor(wk[:, 1:K + 1, :], wk[:, 1:K + 1, :], wk2[:, :, :], ALU.subtract).then_inc(wk_ready, 1)
            for b, taps, psum in tap_banks():
                dve.wait_ge(cwh_ready, b + 1)
                dve.tensor_tensor(cwl[:, taps, :], psum, cwh[:, taps, :].bitcast(F32), ALU.subtract)\
                    .then_inc(cwl_ready, 1)

            def split_layer_weights():
                dve.wait_ge(layer_in, ALL_LAYER)
                dve.wait_ge(vcol_done, 1)
                dve.tensor_copy(vcol[:, :], bank[6][:, 0:NV]).then_inc(vcol_ready, 1)
                dve.wait_ge(vcol_ready, 1)
                for l in range(NL):
                    link(dve.tensor_scalar(inf[:, l, :], inw[:, l, :], lnw[:, l:l + 1], None, ALU.mult))
                link(dve.tensor_copy(inh[:, :, :], inf[:, :, :]))
                dve.tensor_tensor(inl[:, :, :], inf[:, :, :], inh[:, :, :].bitcast(F32), ALU.subtract)
                dve.wait_ge(xpT_done, 1)
                dve.tensor_copy(xpT[:, :, :], bank[5][0:RK, 0:NL * DI].rearrange("r (l d) -> r l d", l=NL))\
                    .then_inc(xpT_ready, 1)

            def layer_biases():
                dve.wait_ge(inbias_done, 1)
                link(dve.tensor_tensor(inb[:, :, :], inb[:, :, :],
                                       bank[4][:, 0:2 * NL].rearrange("d (l h) -> d l h", l=NL), ALU.add))
                link(dve.tensor_copy(bias_g[:, :], inb[:, :, 1]))
                link(dve.tensor_tensor(bias_s[:, :], inb[:, :, 0], tapw[:, :], ALU.mult))
                link(dve.tensor_tensor(bias_x[:, :], bias_s[:, :], tapb[:, :], ALU.add))
                dve.wait_ge(wdt_done, 1)
                wdt = bank[7][:, 0:NL * DI].rearrange("r (l d) -> r l d", l=NL)
                link(dve.tensor_copy(wdth[:, :, :], wdt))
                dve.tensor_tensor(wdtl[:, :, :], wdt, wdth[:, :, :].bitcast(F32), ALU.subtract)\
                    .then_inc(layers_ready, 1)

            def split_expert_weights():
                dve.wait_ge(expert_in, ALL_EXPERT)
                link(dve.tensor_copy(w1h[:, :, :], w1f[:, :, :]))
                dve.tensor_tensor(w1l[:, :, :], w1f[:, :, :], w1h[:, :, :].bitcast(F32), ALU.subtract)
                link(dve.tensor_copy(b2h[:, :, :], b2d[:, :, :]))
                dve.tensor_tensor(b2l[:, :, :], b2d[:, :, :], b2h[:, :, :].bitcast(F32), ALU.subtract)
                link(dve.tensor_copy(gw2[:, 0, :], gwf[:, :]))
                dve.tensor_tensor(gw2[:, 1, :], gwf[:, :], gw2[:, 0, :].bitcast(F32), ALU.subtract)\
                    .then_inc(experts_ready, 1)

            def td(a):
                return a.rearrange("u (n d) -> u n d", d=D)

            def bcast(a, w=D):
                return a.rearrange("u (n a) -> u n a", a=1).broadcast_to([U, NB, w])

            def head_lo(c):
                dve.wait_ge(xh_ready, c + 1)
                reuse(dve, conv_done, c)
                dve.tensor_tensor(xl[:, :, 0:UI], HEAD[:, 0:G * UI].rearrange("p (g v) -> p g v", g=G),
                                  xh[:, :, 0:UI].bitcast(F32), ALU.subtract).then_inc(xl_ready, 1)

            def ln_center(i, c):
                src = z[i - 1] if i else ct
                if i == 0:
                    dve.wait_ge(c_saved, c + 1)
                    reuse(dve, base_part[0], c)
                else:
                    dve.wait_ge(z_ready[i - 1], c + 1)
                reuse(dve, ln_d[i], c)
                dve.reduce_sum(lnsum[:, i, :], td(src[:, :]), AX.X).then_inc(ln_sum[i], 1)
                dve.wait_ge(ln_sum[i], c + 1)
                reuse(dve, ln_sq[i], c)
                reuse(dve, ln_a[i], c)
                reuse(dve, ln_hi[i], c)
                dve.scalar_tensor_tensor(td(lnd[:, i, :]), bcast(lnsum[:, i, :]), -1.0 / D, td(src[:, :]),
                                         ALU.mult, ALU.add).then_inc(ln_d[i], 1)

            def ln_variance(i, c):
                dve.wait_ge(ln_sq[i], c + 1)
                reuse(dve, ln_r[i], c)
                if i == 0:
                    reuse(dve, outer_r, c)
                dve.reduce_sum(lnvar[:, i, :], td(lnsq[:, i, :]), AX.X).then_inc(ln_var[i], 1)
                dve.wait_ge(ln_var[i], c + 1)
                if i:
                    dve.tensor_scalar(lnve[:, i, :], lnvar[:, i, :], 1.0 / D, EPS, ALU.mult, ALU.add)\
                        .then_inc(ln_ve[i], 1)
                    return
                dve.tensor_scalar(lnve[:, OUTER, :], lnvar[:, i, :], 1.0 / D, EPS, ALU.mult, ALU.add)
                dve.tensor_scalar(lnve[:, i, :], lnvar[:, i, :], (1.0 + EPS) / D, EPS * EPS, ALU.mult, ALU.add)\
                    .then_inc(ln_ve[i], 1)

            def ln_scale(i, c):
                dve.wait_ge(ln_r[i], c + 1)
                reuse(dve, ln_lo[i], c)
                dve.tensor_tensor(td(lna[:, i, :]), td(lnd[:, i, :]), bcast(lnr[:, i, :]),
                                  ALU.mult).then_inc(ln_a[i], 1)

            def ln_split(i, c):
                dve.wait_ge(ln_hi[i], c + 1)
                dve.wait_ge(ln_a[i], c + 1)
                reuse(dve, t2_done[i], 2 * c)
                dve.tensor_tensor(lhl[:, i, :, D:2 * D], td(lna[:, i, :]), lhl[:, i, :, 0:D],
                                  ALU.subtract).then_inc(ln_lo[i], 1)

            def at_first(i, c):
                dve.wait_ge(t2_done[i], 2 * c + 1)
                if i < 2:
                    reuse(dve, in_done[i], 4 * c)
                else:
                    reuse(dve, hid_done, 2 * E * c)
                    reuse(dve, gate_done, c)
                dve.tensor_copy(at[i][:, 0:HALF], src_of(i)[0][:, 0:HALF]).then_inc(at_a[i], 1)

            def conv_hi(l, c):
                for h in range(2):
                    cols = slice(h * HALF, (h + 1) * HALF)
                    dve.wait_ge(xc_ready[l], 2 * c + h + 1)
                    reuse(dve, dt_done[l], 2 * c)
                    reuse(dve, xcl_ready[l], 2 * c)
                    dve.tensor_copy(xch[l][:, cols], xc[l][:, cols]).then_inc(xch_ready[l], 1)

            def states(l, c):
                for h in range(2):
                    dve.wait_ge(bm_ready[l], 2 * c + h + 1)
                    reuse(dve, bc_ready[l], c)
                    dve.tensor_tensor(bcp[l][:, h * G:(h + 1) * G, :],
                                      RING[l][h][0:U, :].rearrange("u (n s) -> u n s", n=G)[:, :, DS:2 * DS],
                                      bm[l][:, h * G:(h + 1) * G, :], ALU.mult).then_inc(bcp_ready[l], 1)
                dve.wait_ge(bcp_ready[l], 2 * c + 2)
                reuse(dve, spread_done[l], 2 * c)
                dve.reduce_sum(bc[l][:, :], bcp[l][:, :, :], AX.X).then_inc(bc_ready[l], 1)

            def clamp(l, c):
                for h in range(2):
                    cols = slice(h * HALF, (h + 1) * HALF)
                    dve.wait_ge(ex_ready[l], 2 * c + h + 1)
                    dve.tensor_scalar(ex[l][:, cols], ex[l][:, cols], SOFTPLUS_CAP, None, ALU.min)\
                        .then_inc(exc_ready[l], 1)

            def steps_of_time(l, c):
                for h in range(2):
                    cols = slice(h * HALF, (h + 1) * HALF)
                    dve.wait_ge(lg_ready[l], 2 * c + h + 1)
                    reuse(dve, o_done[l], c)
                    dve.scalar_tensor_tensor(dt[l][:, cols], RING[l][h][:, 0:HALF], dpb[:, l:l + 1], ex[l][:, cols],
                                             ALU.add, ALU.max).then_inc(dt_ready[l], 1)

            def through_state(l, c):
                for h in range(2):
                    cols = slice(h * HALF, (h + 1) * HALF)
                    dve.wait_ge(spread_done[l], 2 * c + h + 1)
                    dve.wait_ge(dt_ready[l], 2 * c + h + 1)
                    dve.tensor_tensor(dt[l][:, cols], RING[l][h][:, 0:HALF], dt[l][:, cols], ALU.mult)\
                        .then_inc(dbc_ready[l], 1)
                for h in range(2):
                    cols = slice(h * HALF, (h + 1) * HALF)
                    dve.wait_ge(dbc_ready[l], 2 * c + h + 1)
                    dve.wait_ge(u0_ready[l], 2 * c + h + 1)
                    dve.scalar_tensor_tensor(dt[l][:, cols], dt[l][:, cols], dpar[:, l:l + 1], u0[l][:, cols],
                                             ALU.add, ALU.mult).then_inc(u1_ready[l], 1)

            def layer_out(l, c):
                dve.wait_ge(o_done[l], c + 1)
                dve.wait_ge(base_ready[l], c + 1)
                reuse(dve, ln_d[l + 1], c)
                if l == 0:
                    reuse(dve, base_ready[1], c)
                else:
                    reuse(dve, acc_init, c)
                dve.tensor_tensor(z[l][:, :], RING[l][0][0:U, :], base[:, l, :], ALU.add).then_inc(z_ready[l], 1)

            NGS = 16
            at_step = [0]

            def gate_link(c, ins):
                at_step[0] += 1
                ins.then_inc(gate_step, 1)
                dve.wait_ge(gate_step, c * NGS + at_step[0])

            def spread(a):
                return bcast(a[:, :], E)

            def gate_pick(c):
                ranks = rank[:, :].rearrange("u (a e) -> u a e", a=1).broadcast_to([U, NB, E])
                at_step[0] = 0
                dve.wait_ge(gate_done, c + 1)
                logits = YB[0:U, 0:2 * NB * E].rearrange("u (n k e) -> u k n e", k=2, e=E)
                gate_link(c, dve.tensor_tensor(lgh[:, :, :], logits[:, 0],
                                               gbr[:, :].rearrange("u (a e) -> u a e", a=1).broadcast_to([U, NB, E]),
                                               ALU.add))
                gate_link(c, dve.tensor_tensor(lgt[:, :, :], logits[:, 1], lgh[:, :, :], ALU.add))
                gate_link(c, dve.reduce_max(lmx[:, :], lgt[:, :, :], AX.X))
                reuse(dve, lex_ready, c)
                dve.tensor_tensor(lsh[:, :, :], lgt[:, :, :], spread(lmx), ALU.subtract).then_inc(lsh_ready, 1)
                dve.wait_ge(lsh_ready, c + 1)
                gate_link(c, dve.scalar_tensor_tensor(lcd[:, :, :], lsh[:, :, :], 0.0, ranks, ALU.is_equal, ALU.mult))
                gate_link(c, dve.reduce_max(lkx[:, :], lcd[:, :, :], AX.X))
                gate_link(c, dve.tensor_tensor(lhot[:, :, :], lcd[:, :, :], spread(lkx), ALU.is_equal))
                gate_link(c, dve.scalar_tensor_tensor(lg2[:, :, :], lhot[:, :, :], LOGIT_DROP, lsh[:, :, :],
                                                      ALU.mult, ALU.add))
                gate_link(c, dve.reduce_max(lmx2[:, :], lg2[:, :, :], AX.X))
                gate_link(c, dve.tensor_tensor(leq2[:, :, :], lg2[:, :, :], spread(lmx2), ALU.is_equal))
                gate_link(c, dve.tensor_tensor(lcd2[:, :, :], leq2[:, :, :], ranks, ALU.mult))
                gate_link(c, dve.reduce_max(lkx2[:, :], lcd2[:, :, :], AX.X))
                gate_link(c, dve.tensor_tensor(lhot2[:, :, :], lcd2[:, :, :], spread(lkx2), ALU.is_equal))
                dve.tensor_tensor(lsel[:, :, :], lhot[:, :, :], lhot2[:, :, :], ALU.add)

            def gate_weigh(c):
                dve.wait_ge(lex_ready, c + 1)
                gate_link(c, dve.reduce_sum(lsm[:, :], lex[:, :, :], AX.X))
                gate_link(c, dve.reciprocal(lrc[:, :], lsm[:, :]))
                dve.tensor_tensor(lpw[:, :, :], lex[:, :, :], spread(lrc), ALU.mult).then_inc(gate_end, 1)
                dve.wait_ge(gate_end, c + 1)
                reuse(dve, py_ready, E * c)
                gate_link(c, dve.tensor_tensor(wts[:, :, :], lpw[:, :, :], lsel[:, :, :], ALU.mult))
                reuse(dve, cwT_done, c)
                gate_link(c, dve.tensor_copy(cwt[:, :, 0:E].bitcast(F32R), wts[:, :, :]))
                assert at_step[0] == NGS
                dve.tensor_tensor(cwt[:, :, E:EP], wts[:, :, :], cwt[:, :, 0:E], ALU.subtract).then_inc(cw_ready, 1)

            def expert_base(c):
                dve.wait_ge(cwT_done, c + 1)
                reuse(dve, b2_done, c)
                dve.tensor_copy(cwT[:, :], YB[:, 0:U]).then_inc(cwT_ready, 1)

            def product(e, c):
                dve.wait_ge(y_done, c * E + e + 1)
                if e >= NPY:
                    dve.wait_ge(acc_add, c * E + e - NPY + 1)
                else:
                    reuse(dve, acc_add, c * E)
                dve.tensor_tensor(td(py[e % NPY][:, :]), td(YBANK[e % 2][0:U, :]),
                                  wts[:, :, e:e + 1].broadcast_to([U, NB, D]), ALU.mult).then_inc(py_ready, 1)

            def step(h, a, b, f):
                on(f, at_first, 2)
                on(a, conv_hi, 0)
                on(h, head_lo)
                on(b, conv_hi, 1)
                if first(h):
                    split_layer_weights()
                on(f, gate_pick)
                on(a, states, 0)
                on(b, states, 1)
                on(f, gate_weigh)
                on(a, clamp, 0)
                on(b, clamp, 1)
                on(f, expert_base)
                on(a, steps_of_time, 0)
                on(b, steps_of_time, 1)
                on(a, through_state, 0)
                on(b, through_state, 1)
                if first(h):
                    layer_biases()
                on(h, ln_center, 0)
                on(a, layer_out, 0)
                on(a, ln_center, 1)
                on(h, ln_variance, 0)
                on(f, product, 0)
                on(b, layer_out, 1)
                on(a, ln_variance, 1)
                on(b, ln_center, 2)
                on(f, product, 1)
                on(h, ln_scale, 0)
                on(h, ln_split, 0)
                on(f, product, 2)
                on(a, ln_scale, 1)
                on(a, ln_split, 1)
                on(b, ln_variance, 2)
                on(f, product, 3)
                on(h, at_first, 0)
                on(f, product, 4)
                on(a, at_first, 1)
                on(b, ln_scale, 2)
                on(b, ln_split, 2)
                on(f, product, 5)
                on(f, product, 6)
                on(f, product, 7)
                if first(h):
                    split_expert_weights()

            run_steps(dve, step)

        @block.tensor
        def _(pe):
            pe.wait_ge(s_id, 2)
            pe.wait_ge(wk_ready, 1)
            for b, taps, _ in tap_banks():
                for j in range(taps.start, taps.stop):
                    for p in range(2):
                        mm = pe.transpose(bank[1 + b][:, (j % 4) * 128 + p * COUT:(j % 4) * 128 + (p + 1) * COUT],
                                          wk[:, 2 * j + 1 - p:2 * j + 3 - p, :].rearrange("o k i -> o (k i)"),
                                          ident[0:COUT, 0:COUT])
                mm.then_inc(cwp_done, 1)

            def vectors_to_columns():
                pe.wait_ge(layer_in, ALL_LAYER)
                pe.transpose(bank[6][:, 0:NV], vrow[:, :], ident[0:NV, 0:NV]).then_inc(vcol_done, 1)
                for l in range(NL):
                    mm = pe.transpose(bank[5][0:RK, l * DI:(l + 1) * DI], xpw[:, l, 0:RK], ident[:, :])
                mm.then_inc(xpT_done, 1)

            def fold_layer_weights():
                pe.wait_ge(vcol_ready, 1)
                for l in range(NL):
                    for h in range(2):
                        mm = pe.matmul(bank[4][:, 2 * l + h:2 * l + h + 1], inw[0:D, l, h * DI:(h + 1) * DI],
                                       lnb[0:D, l:l + 1], start=True, stop=True)
                mm.then_inc(inbias_done, 1)
                pe.wait_ge(xpT_ready, 1)
                for l in range(NL):
                    mm = pe.matmul(bank[7][:, l * DI:(l + 1) * DI], xpT[:, l, :], dpw[:, l, :],
                                   start=True, stop=True)
                mm.then_inc(wdt_done, 1)

            def cols(n):
                return slice(n * U, (n + 1) * U)

            def transpose_x(c):
                pe.wait_ge(s_x, 16 * (c + 1))
                reuse(pe, c_saved, c)
                if not isinstance(c, int) or c > 3:
                    pe.wait_ge(py_ready, E * (c - 3))
                for g in range(G):
                    mm = pe.transpose(HEAD[:, g * UI:(g + 1) * UI], xs[:, g, :], ident[0:UI, 0:UI])
                mm.then_inc(xt_ready, 1)

            def conv(part, c):
                w, v = ((cwh, xh), (cwl, xh), (cwh, xl))[part]
                if part == 0:
                    pe.wait_ge(xl_ready, c + 1)
                if first(c):
                    pe.wait_ge([cwh_ready, cwl_ready, cwl_ready][part], (JT + 3) // 4)
                for j in range(JT):
                    mm = pe.matmul(HEAD[:, 0:G * U], w[:, j, :], v[:, :, j:j + U],
                                   start=(part == 0 and j == 0), stop=(part == 2 and j == JT - 1))
                if part == 2:
                    mm.then_inc(conv_done, 1)

            def transpose_c(c):
                pe.wait_ge(cf_ready, c + 1)
                for g in range(G):
                    mm = pe.transpose(HEAD[0:U, g * 128:(g + 1) * 128], cf[:, g, :], ident[:, :])
                mm.then_inc(t1_done, 1)

            def transpose_rows(i, c):
                to = src_of(i)
                pe.wait_ge(ln_lo[i], c + 1)
                for h in range(2):
                    if i < 2:
                        reuse(pe, [z_ready[i], dbc_ready[i]][h], c * (1 + h))
                    else:
                        reuse(pe, gelu_done, 2 * E * c)
                    for n in range(G):
                        mm = pe.transpose(to[h][:, cols(n)], lhl[:, i, h * G + n, :], ident[0:U, 0:U])
                    mm.then_inc(t2_done[i], 1)

            def project_in(l, m, c):
                for h in range(2):
                    if m:
                        pe.wait_ge(xc_ready[l], 2 * c + h + 1)
                    else:
                        pe.wait_ge([at_a, at_b][h][l], c + 1)
                    for n, w in enumerate((inh, inl)):
                        mm = pe.matmul(RING[l][h][:, 0:HALF], w[:, l, m * DI:(m + 1) * DI],
                                       at[l][:, h * HALF:(h + 1) * HALF], start=(n == 0), stop=(n == 1))
                    mm.then_inc(in_done[l], 1)

            def project_states(l, c):
                pe.wait_ge(xc_ready[l], 2 * c + 2)
                for h in range(2):
                    pe.wait_ge(sg_ready[l], 2 * c + h + 1)
                    for n in range(G):
                        mm = pe.matmul(RING[l][h][0:U, n * 128:(n + 1) * 128], xc[l][:, cols(h * G + n)],
                                       xpw[:, l, RK:RK + 2 * DS], start=True, stop=True)
                    mm.then_inc(bc_done[l], 1)

            def project_dt(l, c):
                for h in range(2):
                    pe.wait_ge(bcp_ready[l], 2 * c + h + 1)
                    pe.wait_ge(xcl_ready[l], 2 * c + h + 1)
                    for n, (w, v) in enumerate(((wdth, xch), (wdtl, xch), (wdth, xcl))):
                        mm = pe.matmul(RING[l][h][:, 0:HALF], w[:, l, :], v[l][:, h * HALF:(h + 1) * HALF],
                                       start=(n == 0), stop=(n == 2))
                    mm.then_inc(dt_done[l], 1)

            def spread_states(l, c):
                for h in range(2):
                    pe.wait_ge(dt_ready[l], 2 * c + h + 1)
                    pe.wait_ge(bc_ready[l], c + 1)
                    for n in range(h * G, (h + 1) * G):
                        mm = pe.transpose(RING[l][h][:, cols(n - h * G)], bc[l][:, n:n + 1].broadcast_to([U, DI]),
                                          ident[0:U, 0:U])
                    mm.then_inc(spread_done[l], 1)

            def project_out(l, c):
                pe.wait_ge(dbc_ready[l], 2 * c + 1)
                pe.wait_ge(u1_ready[l], 2 * c + 2)
                for n in range(NB):
                    mm = pe.matmul(RING[l][0][0:U, n * D:(n + 1) * D], dt[l][:, cols(n)], ow[:, l, :],
                                   start=True, stop=True)
                mm.then_inc(o_done[l], 1)

            def gate(c):
                if first(c):
                    pe.wait_ge(experts_ready, 1)
                pe.wait_ge(at_a[2], c + 1)
                pe.wait_ge(at_b[2], c + 1)
                reuse(pe, py_ready, E * c)
                for n in range(NB):
                    mm = pe.matmul(YB[0:U, n * 2 * E:(n + 1) * 2 * E], at[2][:, cols(n)],
                                   gw2[:, :, :].rearrange("d k e -> d (k e)"), start=True, stop=True)
                mm.then_inc(gate_done, 1)

            def expert_weights(c):
                pe.wait_ge(cw_ready, c + 1)
                pe.transpose(YB[:, 0:U], cwt[:, :, :].rearrange("u n e -> u (n e)"), ident[0:U, 0:U])\
                    .then_inc(cwT_done, 1)

            def expert_bias(c):
                pe.wait_ge(cwT_ready, c + 1)
                for k, b in enumerate((b2h, b2l)):
                    mm = pe.matmul(YB[0:U, :], cwT[:, :], b[:, :, :].rearrange("k n d -> k (n d)"),
                                   start=(k == 0), stop=(k == 1))
                mm.then_inc(b2_done, 1)

            def hidden(e, c):
                for h in range(2):
                    if e:
                        pe.wait_ge(gelu_done, 2 * E * c + 2 * e + h - 1)
                    for k, w in enumerate((w1h, w1l)):
                        mm = pe.matmul(HID[h][:, 0:HALF], w[:, e, :], at[2][:, h * HALF:(h + 1) * HALF],
                                       start=(k == 0), stop=(k == 1))
                    mm.then_inc(hid_done, 1)

            def expert_out(e, c, head):
                if e >= 2:
                    pe.wait_ge(py_ready, E * c + e - 1)
                elif e == 0:
                    pe.wait_ge(b2_saved, c + 1)
                elif head is not None:
                    pe.wait_ge(c_saved, head + 1)
                else:
                    reuse(pe, py_ready, E * c)
                pe.wait_ge(gelu_done, 2 * E * c + 2 * e + 2)
                for n in range(NB):
                    mm = pe.matmul(YBANK[e % 2][0:U, n * D:(n + 1) * D], gl[e % 2][:, cols(n)], w2s[:, e, :],
                                   start=True, stop=True)
                mm.then_inc(y_done, 1)

            def experts(e0, e1, c, head):
                for e in range(e0, e1):
                    if e + 1 < E:
                        hidden(e + 1, c)
                    expert_out(e, c, head)

            def step(h, a, b, f):
                on(f, transpose_rows, 2)
                on(h, transpose_x)
                if first(h):
                    vectors_to_columns()
                on(a, project_in, 0, 1)
                on(f, gate)
                on(b, project_in, 1, 1)
                on(h, conv, 0)
                on(a, project_states, 0)
                on(b, project_states, 1)
                on(a, project_dt, 0)
                on(b, project_dt, 1)
                on(h, conv, 1)
                on(f, expert_weights)
                on(h, conv, 2)
                on(a, spread_states, 0)
                on(f, expert_bias)
                on(b, spread_states, 1)
                on(f, hidden, 0)
                if first(h):
                    fold_layer_weights()
                on(h, transpose_c)
                on(a, project_out, 0)
                on(b, project_out, 1)
                if f is not None:
                    experts(0, 4, f, h)
                on(h, transpose_rows, 0)
                if f is not None:
                    experts(4, 5, f, h)
                if first(h):
                    pe.wait_ge(layers_ready, 1)
                on(h, project_in, 0, 0)
                on(a, transpose_rows, 1)
                if f is not None:
                    experts(5, 6, f, h)
                on(a, project_in, 1, 0)
                if f is not None:
                    experts(6, 8, f, h)

            run_steps(pe, step)


_INS = ['x', 'L0_tok_w_real', 'L0_tok_w_imag', 'L0_tok_phases', 'L0_attn_ln_w', 'L0_attn_ln_b', 'L0_attn_in_w',
        'L0_attn_in_b', 'L0_attn_conv_w', 'L0_attn_conv_b', 'L0_attn_xproj_w', 'L0_attn_dtproj_w',
        'L0_attn_dtproj_b', 'L0_attn_D_param', 'L0_attn_out_w', 'L0_attn_out_b', 'L0_ffn_gate_w',
        'L0_ffn_gate_b', 'L0_ffn_W1', 'L0_ffn_b1', 'L0_ffn_W2', 'L0_ffn_b2']
_OUTS = [((64, 235, 64), 'float32')]


def kernel(**inputs):
    import numpy as _np
    import concourse.bacc as _bacc
    from concourse import mybir as _mybir
    from concourse.bass_utils import run_bass_kernel_spmd as _run

    nc = _bacc.Bacc("TRN2", target_bir_lowering=False, num_devices=1)
    arrays, args = {}, []
    for name in _INS:
        a = _np.ascontiguousarray(inputs[name])
        arrays[f"in_{name}_dram"] = a
        args.append(nc.dram_tensor(f"in_{name}_dram", a.shape, _mybir.dt.from_np(a.dtype), kind="ExternalInput").ap())
    for i, (shape, dtype) in enumerate(_OUTS):
        dt = _mybir.dt.from_np(_np.dtype(dtype))
        args.append(nc.dram_tensor(f"out_{i}_dram", shape, dt, kind="ExternalOutput").ap())
    audio_tower(nc, *args)
    r = _run(nc, [arrays], core_ids=[0])
    got = tuple(r.results[0][f"out_{i}_dram"] for i in range(len(_OUTS)))
    return got[0]
```
